# Optimizing a Trainium2 kernel written in Bass

```python
import numpy as np
import jax
import jax.numpy as jnp

def _softmax(x, axis=-1):
    return jax.nn.softmax(x, axis=axis)

def _gelu(x):
    return jax.nn.gelu(x, approximate=True)

def _silu(x):
    return jax.nn.silu(x)

def _sigmoid(x):
    return jax.nn.sigmoid(x)

def _layernorm(x, axis=-1, eps=1e-05):
    m = jnp.mean(x, axis=axis, keepdims=True)
    v = jnp.var(x, axis=axis, keepdims=True)
    return (x - m) / jnp.sqrt(v + eps)

def _scatter_add(tgt, idx, src, axis=0):
    return tgt.at[idx].add(src)

def _segment_sum(src, seg, n):
    return jax.ops.segment_sum(src, seg, n)
kernel_name = 'mk_gnn_resnorm_d2_gnn_r8_d932fc'

def setup_inputs(seed: int=0):
    np.random.seed(seed)
    _w = jnp.asarray

    def _rec_inputs():
        import jax
        import jax.numpy as jnp
        _gk = jax.random.key(seed)
        x = -0.0003713 + 1 * jax.random.normal(jax.random.fold_in(_gk, 1), (12500, 128), jnp.float32)
        _s = jax.random.randint(jax.random.fold_in(_gk, 2), (100000,), 0, 12500, jnp.int32)
        _d = jax.random.randint(jax.random.fold_in(_gk, 3), (100000,), 0, 12500, jnp.int32)
        _loop = jnp.arange(12500, dtype=jnp.int32)
        src = jnp.concatenate([_s, _d, _loop])
        dst = jnp.concatenate([_d, _s, _loop])
        _o = jnp.argsort(dst, stable=True)
        src = src[_o]
        dst = dst[_o]
        edge_type_9 = jax.random.randint(jax.random.fold_in(_gk, 12), (212500,), 0, 9, jnp.int32)
        return (x, src, dst, edge_type_9)
    x, src, dst, edge_type_9 = _rec_inputs()

    def _L0_gnn_setup():
        import jax, jax.numpy as jnp
        import numpy as np
        N_NODES = 12500
        N_EDGES = 75000
        H = 128
        NUM_STEPS = 5
        key = jax.random.key(seed)
        ks = jax.random.split(key, 8)
        s = 0.05
        return {'x': jax.random.normal(ks[0], (N_NODES, H), dtype=jnp.float32), 'edge_index': jax.random.randint(ks[1], (2, N_EDGES), 0, N_NODES, dtype=jnp.int64), 'W_msg': jax.random.normal(ks[2], (H, H), dtype=jnp.float32) * s, 'b_msg': jax.random.normal(ks[3], (H,), dtype=jnp.float32) * s, 'W_ih': jax.random.normal(ks[4], (3 * H, H), dtype=jnp.float32) * s, 'W_hh': jax.random.normal(ks[5], (3 * H, H), dtype=jnp.float32) * s, 'b_ih': jax.random.normal(ks[6], (3 * H,), dtype=jnp.float32) * s, 'b_hh': jax.random.normal(ks[7], (3 * H,), dtype=jnp.float32) * s}
    _L0_gnn_all = _L0_gnn_setup()
    _L0_gnn_in = {k: v for k, v in _L0_gnn_all.items() if k in ('W_msg', 'b_msg', 'W_ih', 'W_hh', 'b_ih', 'b_hh')}
    del _L0_gnn_all

    def _L1_gnn_setup():
        import jax, jax.numpy as jnp
        import numpy as np
        NUM_EDGE_TYPES = 8
        HIDDEN = 128
        N_NODES = 6250
        N_EDGES = 75000

        def _gru_cell(x, h, W_ih, W_hh, b_ih, b_hh):
            H = h.shape[-1]
            gi = x @ W_ih.T + b_ih
            gh = h @ W_hh.T + b_hh
            i_r, i_z, i_n = (gi[:, :H], gi[:, H:2 * H], gi[:, 2 * H:])
            h_r, h_z, h_n = (gh[:, :H], gh[:, H:2 * H], gh[:, 2 * H:])
            r = jax.nn.sigmoid(i_r + h_r)
            z = jax.nn.sigmoid(i_z + h_z)
            n = jnp.tanh(i_n + r * h_n)
            return (1.0 - z) * n + z * h
        key = jax.random.key(seed)
        ks = jax.random.split(key, 10)
        H = HIDDEN
        h = jax.random.normal(ks[0], (N_NODES, H), dtype=jnp.float32)
        edge_index = jax.random.randint(ks[1], (2, N_EDGES), 0, N_NODES, dtype=jnp.int32)
        edge_type = jax.random.randint(ks[2], (N_EDGES,), 0, NUM_EDGE_TYPES + 1, dtype=jnp.int32)
        s = 1.0 / np.sqrt(H)
        W_msg = jax.random.uniform(ks[3], (H, H), jnp.float32, -s, s)
        b_msg = jax.random.uniform(ks[4], (H,), jnp.float32, -s, s)
        edge_embed = jax.random.normal(ks[5], (NUM_EDGE_TYPES + 1, H), dtype=jnp.float32)
        W_ih = jax.random.uniform(ks[6], (3 * H, H), jnp.float32, -s, s)
        W_hh = jax.random.uniform(ks[7], (3 * H, H), jnp.float32, -s, s)
        b_ih = jax.random.uniform(ks[8], (3 * H,), jnp.float32, -s, s)
        b_hh = jax.random.uniform(ks[9], (3 * H,), jnp.float32, -s, s)
        return {'h': h, 'edge_index': edge_index, 'edge_type': edge_type, 'num_nodes': N_NODES, 'W_msg': W_msg, 'b_msg': b_msg, 'edge_embed': edge_embed, 'W_ih': W_ih, 'W_hh': W_hh, 'b_ih': b_ih, 'b_hh': b_hh}
    _L1_gnn_all = _L1_gnn_setup()
    _L1_gnn_in = {k: v for k, v in _L1_gnn_all.items() if k in ('W_msg', 'b_msg', 'edge_embed', 'W_ih', 'W_hh', 'b_ih', 'b_hh')}
    del _L1_gnn_all
    return {'x': x, 'src': src, 'dst': dst, 'edge_type_9': edge_type_9, 'L0_gnn_W_msg': _L0_gnn_in['W_msg'], 'L0_gnn_b_msg': _L0_gnn_in['b_msg'], 'L0_gnn_W_ih': _L0_gnn_in['W_ih'], 'L0_gnn_W_hh': _L0_gnn_in['W_hh'], 'L0_gnn_b_ih': _L0_gnn_in['b_ih'], 'L0_gnn_b_hh': _L0_gnn_in['b_hh'], 'L1_gnn_W_msg': _L1_gnn_in['W_msg'], 'L1_gnn_b_msg': _L1_gnn_in['b_msg'], 'L1_gnn_edge_embed': _L1_gnn_in['edge_embed'], 'L1_gnn_W_ih': _L1_gnn_in['W_ih'], 'L1_gnn_W_hh': _L1_gnn_in['W_hh'], 'L1_gnn_b_ih': _L1_gnn_in['b_ih'], 'L1_gnn_b_hh': _L1_gnn_in['b_hh']}

def reference(x, src, dst, edge_type_9, L0_gnn_W_msg, L0_gnn_b_msg, L0_gnn_W_ih, L0_gnn_W_hh, L0_gnn_b_ih, L0_gnn_b_hh, L1_gnn_W_msg, L1_gnn_b_msg, L1_gnn_edge_embed, L1_gnn_W_ih, L1_gnn_W_hh, L1_gnn_b_ih, L1_gnn_b_hh):
    import jax
    import jax.numpy as jnp

    def _L0_gnn_ref(x, edge_index, W_msg, b_msg, W_ih, W_hh, b_ih, b_hh):
        import jax, jax.numpy as jnp
        import numpy as np
        N_NODES = 12500
        N_EDGES = 75000
        H = 128
        NUM_STEPS = 5
        num_nodes = x.shape[0]
        row, col = (edge_index[0], edge_index[1])

        def step(h, _):
            messages = h[col] @ W_msg.T + b_msg
            agg = jax.ops.segment_sum(messages, row, num_segments=num_nodes)
            gi = agg @ W_ih.T + b_ih
            gh = h @ W_hh.T + b_hh
            i_r, i_z, i_n = jnp.split(gi, 3, axis=-1)
            h_r, h_z, h_n = jnp.split(gh, 3, axis=-1)
            r = jax.nn.sigmoid(i_r + h_r)
            z = jax.nn.sigmoid(i_z + h_z)
            n = jnp.tanh(i_n + r * h_n)
            h_new = (1.0 - z) * n + z * h
            return (h_new, None)
        h, _ = jax.lax.scan(step, x, None, length=NUM_STEPS)
        return h

    def _L1_gnn_ref(h, edge_index, edge_type, num_nodes, W_msg, b_msg, edge_embed, W_ih, W_hh, b_ih, b_hh):
        import jax, jax.numpy as jnp
        import numpy as np
        NUM_EDGE_TYPES = 8
        HIDDEN = 128
        N_NODES = 6250
        N_EDGES = 75000

        def _gru_cell(x, h, W_ih, W_hh, b_ih, b_hh):
            H = h.shape[-1]
            gi = x @ W_ih.T + b_ih
            gh = h @ W_hh.T + b_hh
            i_r, i_z, i_n = (gi[:, :H], gi[:, H:2 * H], gi[:, 2 * H:])
            h_r, h_z, h_n = (gh[:, :H], gh[:, H:2 * H], gh[:, 2 * H:])
            r = jax.nn.sigmoid(i_r + h_r)
            z = jax.nn.sigmoid(i_z + h_z)
            n = jnp.tanh(i_n + r * h_n)
            return (1.0 - z) * n + z * h
        src = edge_index[0]
        dst = edge_index[1]
        src_h = h[src] @ W_msg.T + b_msg
        emb = edge_embed[jnp.clip(edge_type, 0, NUM_EDGE_TYPES)]
        msg = src_h + emb
        messages = jax.ops.segment_sum(msg, dst, num_segments=num_nodes)
        h_new = _gru_cell(messages, h[:num_nodes], W_ih, W_hh, b_ih, b_hh)
        result = jnp.zeros_like(h).at[:num_nodes].set(h_new)
        return result
    edge_index = jnp.stack([src, dst])
    x = _layernorm(x + _L0_gnn_ref(x, edge_index, L0_gnn_W_msg, L0_gnn_b_msg, L0_gnn_W_ih, L0_gnn_W_hh, L0_gnn_b_ih, L0_gnn_b_hh), axis=-1)
    x = _layernorm(x + _L1_gnn_ref(x, edge_index, edge_type_9, 12500, L1_gnn_W_msg, L1_gnn_b_msg, L1_gnn_edge_embed, L1_gnn_W_ih, L1_gnn_W_hh, L1_gnn_b_ih, L1_gnn_b_hh), axis=-1)
    return x

_drawn_inputs = setup_inputs


def setup_inputs(seed=0):
    import zlib

    import numpy as np

    out = dict(_drawn_inputs(seed))
    spreads = {}
    factors = {'L1_gnn_b_ih': 7.033, 'L1_gnn_b_hh': 8.0}
    for name, (base, spread) in spreads.items():
        noise = np.random.default_rng([zlib.crc32(name.encode()), seed]).standard_normal(out[name].shape)
        drawn = base * np.exp(spread * noise) if base else spread * noise
        out[name] = jnp.asarray(drawn.astype(out[name].dtype))
    for name, factor in factors.items():
        out[name] = (out[name] * factor).astype(out[name].dtype)
    return out
```

```python
from contextlib import ExitStack

import concourse.bass as bass
from concourse import mybir

ALU = mybir.AluOpType
ACT = mybir.ActivationFunctionType
F32 = mybir.dt.float32
I32 = mybir.dt.int32
U32 = mybir.dt.uint32

NODES = 12500
EDGES = 212500
H = 128
TYPES = 9
TC = 16
NT = 125
NTILES = NODES // NT
WT = 4
WN = NT * WT
WINDOWS = NODES // WN
EC = 125
CHUNKS = EDGES // EC
STEPS = 5
EPS = 1e-5
FAR = 1 << 20


def gnn_kernel(nc, x, src, dst, etype, W0, W1, b0, b1, bm0, bm1, emb, out):
    with ExitStack() as ctx:
        def sb(name, shape, dt=F32):
            return ctx.enter_context(nc.sbuf_tensor(name, shape, dt))

        def psum(name, shape, dt=F32):
            return ctx.enter_context(nc.psum_tensor(name, shape, dt))

        def sem(name):
            return ctx.enter_context(nc.semaphore(name))

        rows = nc.dram_tensor("state", [NODES, H], F32, kind="Internal").ap()
        sums = nc.dram_tensor("edge_sums", [NODES, H + TC], F32, kind="Internal").ap()

        ident = sb("ident", [128, 128])
        lower = sb("lower", [EC, EC])
        zeros = sb("zeros", [NT, H + TC])
        iota_t = sb("iota_t", [EC, TC])
        iota_i = sb("iota_i", [128, 128], I32)
        w_sb = sb("w_sb", [H, 2, 7 * H])
        b_sb = sb("b_sb", [H, 2, 7])
        emb_sb = sb("emb_sb", [TC, 2, H])
        bm_sb = sb("bm_sb", [TC, 2, H])
        src_sb = sb("src_sb", [EC, CHUNKS], I32)
        dst_sb = sb("dst_sb", [EC, CHUNKS], I32)
        typ_sb = sb("typ_sb", [EC, CHUNKS], I32)
        typ_f = sb("typ_f", [EC, CHUNKS])

        in_row = sb("in_row", [EC, 1], U32)
        out_row = sb("out_row", [EC, 1], U32)
        out_f = sb("out_f", [EC, 1])
        write_f = sb("write_f", [EC, 1])
        write_row = sb("write_row", [EC, 1], U32)
        same = sb("same", [EC, EC])
        scrap = sb("scrap", [EC, EC])
        dups = sb("dups", [EC, 1])
        msg = sb("msg", [EC, H + TC])
        msg_rows = sb("msg_rows", [EC, H])
        acc = sb("acc", [EC, H + TC])

        s_rows = sb("s_rows", [NT, WT, H + TC])
        h_rows = sb("h_rows", [NT, WT, H])
        hT = sb("hT", [H, WN])
        sT = sb("sT", [H, WN])
        cT = sb("cT", [TC, WN])
        agg = sb("agg", [H, WN])
        r_g = sb("r_g", [H, WN])
        z_g = sb("z_g", [H, WN])
        n_g = sb("n_g", [H, WN])
        t_g = sb("t_g", [H, WN])
        d_g = sb("d_g", [H, WN])
        new_T = sb("new_T", [H, WN])
        res = sb("res", [NT, WT, H])
        new_rows = sb("new_rows", [NT, WT, H])
        stats = sb("stats", [NT, WT, 6])
        mv = sb("mv", [NT, WT, 2])
        var = sb("var", [NT, WT])
        std = sb("std", [NT, WT])
        rstd = sb("rstd", [NT, WT])

        banks = [psum(f"bank{i}", [128, 512]) for i in range(8)]

        loaded = sem("loaded")
        consts = sem("consts")
        vc = sem("vc")
        emb_zero = sem("emb_zero")

        def w_ih(layer, gate):
            return w_sb[:, layer, H * (1 + gate):H * (2 + gate)]

        def w_hh(layer, gate):
            return w_sb[:, layer, H * (4 + gate):H * (5 + gate)]

        with nc.Block() as block:
            @block.sync
            def _(sp):
                for i, W in enumerate((W0, W1)):
                    sp.dma_start(w_sb[:, i, :], W).then_inc(loaded, 16)
                for i, b in enumerate((b0, b1)):
                    sp.dma_start(b_sb[:, i, :], b).then_inc(loaded, 16)
                sp.wait_ge(emb_zero, 1)
                sp.dma_start(emb_sb[0:TYPES, 1, :], emb).then_inc(loaded, 16)
                sp.dma_start(bm_sb[:, 0, :], bm0.to_broadcast([TC, H])).then_inc(loaded, 16)
                sp.dma_start(bm_sb[:, 1, :], bm1.to_broadcast([TC, H])).then_inc(loaded, 16)
                sp.dma_start(src_sb[:, :], src).then_inc(loaded, 16)
                sp.dma_start(dst_sb[:, :], dst).then_inc(loaded, 16)
                sp.dma_start(typ_sb[:, :], etype).then_inc(loaded, 16)
                sp.dma_start(rows, x).then_inc(loaded, 16)
                sp.wait_ge(loaded, 176)

            @block.gpsimd
            def _(pool):
                pool.memset(emb_sb[:, :, :], 0.0).then_inc(emb_zero, 1)
                pool.iota(iota_i[:, :], [[1, 128]], base=0, channel_multiplier=-1).then_inc(consts, 1)

            @block.vector
            def _(dve):
                dve.memset(zeros[:, :], 0.0)
                dve.wait_ge(consts, 1)
                dve.tensor_copy(ident[:, :], iota_i[:, :]).then_inc(vc, 1)
                dve.wait_ge(vc, 1)
                dve.tensor_scalar(lower[:, :], ident[0:EC, 0:EC], 0.0, None, ALU.is_lt).then_inc(vc, 1)
                dve.wait_ge(vc, 2)
                dve.tensor_scalar(ident[:, :], ident[:, :], 0.0, None, ALU.is_equal).then_inc(vc, 1)
                dve.wait_ge(loaded, 176)
                dve.tensor_copy(typ_f[:, :], typ_sb[:, :]).then_inc(vc, 1)
                dve.wait_ge(vc, 4)
                dve.tensor_scalar(typ_f[:, :], typ_f[:, :], 0.0, float(TYPES - 1), ALU.max, ALU.min).then_inc(vc, 1)
                dve.tensor_tensor(b_sb[:, :, 1:3], b_sb[:, :, 1:3], b_sb[:, :, 4:6], ALU.add).then_inc(vc, 1)
                dve.wait_ge(emb_zero, 1)
                dve.tensor_tensor(emb_sb[:, :, :], emb_sb[:, :, :], bm_sb[:, :, :], ALU.add).then_inc(vc, 1)
                dve.wait_ge(vc, 7)

        iota_ready = sem("iota_ready")
        with nc.Block() as block:
            @block.gpsimd
            def _(pool):
                pool.iota(iota_i[0:EC, 0:TC], [[1, TC]], base=0, channel_multiplier=0).then_inc(iota_ready, 1)

            @block.vector
            def _(dve):
                dve.wait_ge(iota_ready, 1)
                dve.tensor_copy(iota_t[:, :], iota_i[0:EC, 0:TC]).then_inc(vc, 1)
                dve.wait_ge(vc, 8)

        def take(eng, sem, n=1):
            eng.wait_ge(sem, n)
            eng.sem_inc(sem, -n)

        (idx_pool, idx_pe, msg_in, acc_in, scattered, acc_done, idx_used, bcast, same_ready, sel_done,
         zeroed, dve_own) = (sem(n) for n in
            ("idx_pool", "idx_pe", "msg_in", "acc_in", "scattered", "acc_done", "idx_used", "bcast",
             "same_ready", "sel_done", "zeroed", "dve_own"))
        sums_clear = sem("sums_clear")

        def sum_edges(layer, in_sb, out_sb):
            with nc.Block() as block:
                @block.sync
                def _(sp):
                    by_tile = sums.rearrange("(a p) f -> a p f", p=NT)
                    with sp.Fori(0, NTILES // 4) as a:
                        for t in range(4):
                            sp.dma_start(by_tile[a * 4 + t], zeros[:, :]).then_inc(zeroed, 16)
                        take(sp, zeroed, 64)
                    sp.sem_inc(sums_clear, 1)

                @block.gpsimd
                def _(pool):
                    take(pool, sums_clear)
                    with pool.Fori(0, CHUNKS):
                        take(pool, idx_pool, 2)
                        pool.indirect_dma_start(msg_rows[:, :], None, rows,
                                                bass.IndirectOffsetOnAxis(ap=in_row[:, :], axis=0)).then_inc(msg_in, 16)
                        pool.indirect_dma_start(acc[:, :], None, sums,
                                                bass.IndirectOffsetOnAxis(ap=out_row[:, :], axis=0)).then_inc(acc_in, 16)
                        take(pool, acc_done, 2)
                        pool.indirect_dma_start(sums, bass.IndirectOffsetOnAxis(ap=write_row[:, :], axis=0),
                                                acc[:, :], None, bounds_check=NODES - 1, oob_is_err=False).then_inc(scattered, 16)
                        pool.wait_ge(scattered, 16)
                        pool.inc_swdge_sem([msg_in, acc_in, scattered], [16, 16, 16], mode="sub")
                        pool.sem_inc(idx_used, 1)

                @block.vector
                def _(dve):
                    dve.sem_inc(idx_used, 1)
                    with dve.Fori(0, CHUNKS) as c:
                        take(dve, idx_used)
                        dve.tensor_copy(out_f[:, :], out_sb[:, bass.ds(c, 1)]).then_inc(idx_pe, 1)
                        dve.tensor_copy(in_row[:, :], in_sb[:, bass.ds(c, 1)]).then_inc(idx_pool, 1)
                        dve.tensor_copy(out_row[:, :], out_sb[:, bass.ds(c, 1)]).then_inc(idx_pool, 1)
                        if layer:
                            dve.tensor_scalar(msg[:, H:H + TC], iota_t[:, :], typ_f[:, bass.ds(c, 1)], None, ALU.is_equal).then_inc(dve_own, 1)
                        else:
                            dve.tensor_scalar(msg[:, H:H + TC], iota_t[:, :], 0.0, None, ALU.is_equal).then_inc(dve_own, 1)
                        take(dve, bcast)
                        dve.tensor_scalar(same[:, :], banks[0][0:EC, 0:EC], out_f[:, :], None, ALU.is_equal).then_inc(dve_own, 1)
                        dve.wait_ge(dve_own, 2)
                        dve.tensor_tensor(scrap[:, :], same[:, :], lower[:, :], ALU.mult).then_inc(dve_own, 1)
                        dve.wait_ge(dve_own, 3)
                        dve.tensor_reduce(dups[:, :], scrap[:, :], mybir.AxisListType.X, ALU.max).then_inc(dve_own, 1)
                        dve.wait_ge(dve_own, 4)
                        dve.scalar_tensor_tensor(out=write_f[:, :], in0=dups[:, :], scalar=float(FAR), in1=out_f[:, :],
                                                 op0=ALU.mult, op1=ALU.add).then_inc(dve_own, 1)
                        take(dve, dve_own, 5)
                        dve.tensor_copy(write_row[:, :], write_f[:, :]).then_inc(acc_done, 1)
                        dve.wait_ge(msg_in, 16)
                        dve.tensor_copy(msg[:, 0:H], msg_rows[:, :]).then_inc(same_ready, 1)
                        take(dve, sel_done)
                        dve.wait_ge(acc_in, 16)
                        dve.tensor_tensor(acc[:, :], acc[:, :], banks[1][0:EC, 0:H + TC], ALU.add).then_inc(acc_done, 1)
                    take(dve, idx_used)

                @block.tensor
                def _(pe):
                    with pe.Fori(0, CHUNKS):
                        take(pe, idx_pe)
                        pe.transpose(banks[0][0:EC, 0:EC], out_f[:, 0:1].to_broadcast([EC, EC]), ident[0:EC, 0:EC]).then_inc(bcast, 1)
                        take(pe, same_ready)
                        pe.matmul(banks[1][0:EC, 0:H + TC], same[:, :], msg[:, :], start=True, stop=True).then_inc(sel_done, 1)

        (win_in, h_in, res_in, turned, s_done, agg_ps, agg_sb, gates_ps, rz_done, pre_n, n_done, new_done, back_ps,
         var_done, std_done, rows_done, stored) = (sem(n) for n in
            ("win_in", "h_in", "res_in", "turned", "s_done", "agg_ps", "agg_sb", "gates_ps", "rz_done", "pre_n", "n_done",
             "new_done", "back_ps", "var_done", "std_done", "rows_done", "stored"))

        def windows(a):
            return a.rearrange("(w t p) f -> w p t f", t=WT, p=NT)

        def gru(L, residual, result):
            with nc.Block() as block:
                @block.sync
                def _(sp):
                    with sp.Fori(0, WINDOWS) as w:
                        sp.dma_start(s_rows[:, :, :], windows(sums)[w]).then_inc(win_in, 16)
                        sp.dma_start(h_rows[:, :, :], windows(rows)[w]).then_inc(h_in, 16)
                        if residual is not None:
                            sp.dma_start(res[:, :, :], windows(residual)[w]).then_inc(res_in, 16)
                        take(sp, rows_done)
                        sp.dma_start(windows(result)[w], new_rows[:, :, :]).then_inc(stored, 16)
                        take(sp, stored, 16)

                @block.tensor
                def _(pe):
                    with pe.Fori(0, WINDOWS):
                        take(pe, win_in, 16)
                        take(pe, h_in, 16)
                        for t in range(WT):
                            node = slice(t * NT, (t + 1) * NT)
                            pe.transpose(banks[0][:, node], s_rows[:, t, 0:H], ident[0:NT, 0:NT])
                            pe.transpose(banks[1][0:TC, node], s_rows[:, t, H:H + TC], ident[0:NT, 0:NT])
                            mm = pe.transpose(banks[7][:, node], h_rows[:, t, :], ident[0:NT, 0:NT])
                        mm.then_inc(turned, 1)
                        take(pe, s_done)
                        pe.matmul(banks[2][:, 0:WN], w_sb[:, L, 0:H], sT[:, :], start=True, stop=False)
                        pe.matmul(banks[2][:, 0:WN], emb_sb[:, L, :], cT[:, :], start=False, stop=True).then_inc(agg_ps, 1)
                        take(pe, agg_sb)
                        for g in range(2):
                            pe.matmul(banks[3 + g][:, 0:WN], w_ih(L, g), agg[:, :], start=True, stop=False)
                            pe.matmul(banks[3 + g][:, 0:WN], w_hh(L, g), hT[:, :], start=False, stop=True)
                        pe.matmul(banks[5][:, 0:WN], w_ih(L, 2), agg[:, :], start=True, stop=True)
                        pe.matmul(banks[6][:, 0:WN], w_hh(L, 2), hT[:, :], start=True, stop=True).then_inc(gates_ps, 1)
                        take(pe, new_done)
                        for t in range(WT):
                            mm = pe.transpose(banks[0][0:NT, t * H:(t + 1) * H], new_T[:, t * NT:(t + 1) * NT], ident[:, :])
                        mm.then_inc(back_ps, 1)

                @block.scalar
                def _(act):
                    with act.Fori(0, WINDOWS):
                        take(act, gates_ps)
                        act.activation(r_g[:, :], banks[3][:, 0:WN], ACT.Sigmoid, bias=b_sb[:, L, 1:2])
                        act.activation(z_g[:, :], banks[4][:, 0:WN], ACT.Sigmoid, bias=b_sb[:, L, 2:3]).then_inc(rz_done, 1)
                        take(act, pre_n)
                        act.activation(n_g[:, :], t_g[:, :], ACT.Tanh, bias=b_sb[:, L, 3:4]).then_inc(n_done, 1)
                        if residual is not None:
                            take(act, var_done)
                            act.activation(std[:, :], var[:, :], ACT.Sqrt).then_inc(std_done, 1)

                @block.vector
                def _(dve):
                    with dve.Fori(0, WINDOWS):
                        take(dve, turned)
                        dve.tensor_copy(sT[:, :], banks[0][:, 0:WN])
                        dve.tensor_copy(hT[:, :], banks[7][:, 0:WN])
                        dve.tensor_copy(cT[:, :], banks[1][0:TC, 0:WN]).then_inc(s_done, 1)
                        take(dve, agg_ps)
                        dve.tensor_copy(agg[:, :], banks[2][:, 0:WN]).then_inc(agg_sb, 1)
                        take(dve, rz_done)
                        dve.scalar_tensor_tensor(out=t_g[:, :], in0=banks[6][:, 0:WN], scalar=b_sb[:, L, 6:7], in1=r_g[:, :],
                                                 op0=ALU.add, op1=ALU.mult).then_inc(dve_own, 1)
                        take(dve, dve_own)
                        dve.tensor_tensor(t_g[:, :], t_g[:, :], banks[5][:, 0:WN], ALU.add).then_inc(pre_n, 1)
                        take(dve, n_done)
                        dve.tensor_tensor(d_g[:, :], hT[:, :], n_g[:, :], ALU.subtract).then_inc(dve_own, 1)
                        take(dve, dve_own)
                        dve.tensor_tensor(d_g[:, :], d_g[:, :], z_g[:, :], ALU.mult).then_inc(dve_own, 1)
                        take(dve, dve_own)
                        dve.tensor_tensor(new_T[:, :], d_g[:, :], n_g[:, :], ALU.add).then_inc(new_done, 1)
                        take(dve, back_ps)
                        back = banks[0][0:NT, 0:WT * H].rearrange("p (t f) -> p t f", t=WT)
                        if residual is None:
                            dve.tensor_copy(new_rows[:, :, :], back).then_inc(rows_done, 1)
                            return
                        take(dve, res_in, 16)
                        dve.tensor_tensor(res[:, :, :], res[:, :, :], back, ALU.add).then_inc(dve_own, 1)
                        take(dve, dve_own)
                        for t in range(WT):
                            last = dve.bn_stats(stats[:, t, :], res[:, t, :])
                        last.then_inc(dve_own, 1)
                        take(dve, dve_own)
                        for t in range(WT):
                            last = dve.bn_aggr(mv[:, t, :], stats[:, t, :])
                        last.then_inc(dve_own, 1)
                        take(dve, dve_own)
                        dve.tensor_scalar(var[:, :], mv[:, :, 1], EPS, None, ALU.add).then_inc(var_done, 1)
                        take(dve, std_done)
                        dve.reciprocal(rstd[:, :], std[:, :]).then_inc(dve_own, 1)
                        take(dve, dve_own)
                        for t in range(WT):
                            last = dve.tensor_scalar(new_rows[:, t, :], res[:, t, :], mv[:, t, 0:1], rstd[:, t:t + 1],
                                                     ALU.subtract, ALU.mult)
                        last.then_inc(rows_done, 1)

        with nc.Fori(0, STEPS - 1):
            sum_edges(0, dst_sb, src_sb)
            gru(0, None, rows)
        sum_edges(0, dst_sb, src_sb)
        gru(0, x, rows)
        sum_edges(1, src_sb, dst_sb)
        gru(1, rows, out)


def kernel(x, src, dst, edge_type_9, L0_gnn_W_msg, L0_gnn_b_msg, L0_gnn_W_ih, L0_gnn_W_hh, L0_gnn_b_ih, L0_gnn_b_hh,
           L1_gnn_W_msg, L1_gnn_b_msg, L1_gnn_edge_embed, L1_gnn_W_ih, L1_gnn_W_hh, L1_gnn_b_ih, L1_gnn_b_hh):
    import numpy as np
    import concourse.bacc as bacc
    from concourse import mybir
    from concourse.bass_utils import run_bass_kernel_spmd

    def weights(msg, ih, hh):
        return np.concatenate([np.asarray(a).T for a in (msg, ih, hh)], axis=1)

    def biases(msg, ih, hh):
        return np.concatenate([np.asarray(a).reshape(-1, H) for a in (msg, ih, hh)]).T

    arrays = {
        "x": np.asarray(x),
        "src": np.asarray(src).reshape(EC, CHUNKS),
        "dst": np.asarray(dst).reshape(EC, CHUNKS),
        "etype": np.asarray(edge_type_9).reshape(EC, CHUNKS),
        "W0": weights(L0_gnn_W_msg, L0_gnn_W_ih, L0_gnn_W_hh),
        "W1": weights(L1_gnn_W_msg, L1_gnn_W_ih, L1_gnn_W_hh),
        "b0": biases(L0_gnn_b_msg, L0_gnn_b_ih, L0_gnn_b_hh),
        "b1": biases(L1_gnn_b_msg, L1_gnn_b_ih, L1_gnn_b_hh),
        "bm0": np.asarray(L0_gnn_b_msg).reshape(1, H),
        "bm1": np.asarray(L1_gnn_b_msg).reshape(1, H),
        "emb": np.asarray(L1_gnn_edge_embed),
    }
    arrays = {f"in_{k}": np.ascontiguousarray(a) for k, a in arrays.items()}
    nc = bacc.Bacc("TRN2", target_bir_lowering=False, num_devices=1)
    args = [nc.dram_tensor(k, a.shape, mybir.dt.from_np(a.dtype), kind="ExternalInput").ap() for k, a in arrays.items()]
    out = nc.dram_tensor("out_0", (NODES, H), mybir.dt.float32, kind="ExternalOutput").ap()
    gnn_kernel(nc, *args, out)
    r = run_bass_kernel_spmd(nc, [arrays], core_ids=[0])
    return r.results[0]["out_0"]
```

```python
from contextlib import ExitStack

import concourse.bass as bass
from concourse import mybir

ALU = mybir.AluOpType
ACT = mybir.ActivationFunctionType
AX = mybir.AxisListType
F32 = mybir.dt.float32
F16 = mybir.dt.float16
F8 = mybir.dt.float8e4
I32 = mybir.dt.int32
U32 = mybir.dt.uint32

NODES = 12500
EDGES = 212500
H = 128
TYPES = 9
TC = 12
NT = 125
NTILES = NODES // NT
WT = 4
WN = NT * WT
WINDOWS = NODES // WN
EC = 125
CHUNKS = EDGES // EC
STEPS = 5
EPS = 1e-5
FAR = 1 << 20

def general_path(nc, x, src, dst, etype, W0, W1, b0, b1, bm0, bm1, emb, out):
    with ExitStack() as ctx:
        def sb(name, shape, dt=F32):
            return ctx.enter_context(nc.sbuf_tensor(name, shape, dt))

        def psum(name, shape, dt=F32):
            return ctx.enter_context(nc.psum_tensor(name, shape, dt))

        def sem(name):
            return ctx.enter_context(nc.semaphore(name))

        rows = nc.dram_tensor("state", [NODES, H], F32, kind="Internal").ap()
        sums = nc.dram_tensor("edge_sums", [NODES, H + TC], F32, kind="Internal").ap()

        ident = sb("ident", [128, 128])
        lower = sb("lower", [EC, EC])
        zeros = sb("zeros", [NT, H + TC])
        iota_t = sb("iota_t", [EC, TC])
        iota_i = sb("iota_i", [128, 128], I32)
        w_sb = sb("w_sb", [H, 2, 7 * H])
        b_sb = sb("b_sb", [H, 2, 7])
        emb_sb = sb("emb_sb", [TC, 2, H])
        bm_sb = sb("bm_sb", [TC, 2, H])
        src_sb = sb("src_sb", [EC, CHUNKS], I32)
        dst_sb = sb("dst_sb", [EC, CHUNKS], I32)
        typ_sb = sb("typ_sb", [EC, CHUNKS], I32)
        typ_f = sb("typ_f", [EC, CHUNKS])

        in_row = sb("in_row", [EC, 1], U32)
        out_row = sb("out_row", [EC, 1], U32)
        out_f = sb("out_f", [EC, 1])
        write_f = sb("write_f", [EC, 1])
        write_row = sb("write_row", [EC, 1], U32)
        same = sb("same", [EC, EC])
        scrap = sb("scrap", [EC, EC])
        dups = sb("dups", [EC, 1])
        msg = sb("msg", [EC, H + TC])
        msg_rows = sb("msg_rows", [EC, H])
        acc = sb("acc", [EC, H + TC])

        s_rows = sb("s_rows", [NT, WT, H + TC])
        h_rows = sb("h_rows", [NT, WT, H])
        hT = sb("hT", [H, WN])
        sT = sb("sT", [H, WN])
        cT = sb("cT", [TC, WN])
        agg = sb("agg", [H, WN])
        r_g = sb("r_g", [H, WN])
        z_g = sb("z_g", [H, WN])
        n_g = sb("n_g", [H, WN])
        t_g = sb("t_g", [H, WN])
        d_g = sb("d_g", [H, WN])
        new_T = sb("new_T", [H, WN])
        res = sb("res", [NT, WT, H])
        new_rows = sb("new_rows", [NT, WT, H])
        stats = sb("stats", [NT, WT, 6])
        mv = sb("mv", [NT, WT, 2])
        var = sb("var", [NT, WT])
        std = sb("std", [NT, WT])
        rstd = sb("rstd", [NT, WT])

        banks = [psum(f"bank{i}", [128, 512]) for i in range(8)]

        loaded = sem("loaded")
        consts = sem("consts")
        vc = sem("vc")
        emb_zero = sem("emb_zero")

        def w_ih(layer, gate):
            return w_sb[:, layer, H * (1 + gate):H * (2 + gate)]

        def w_hh(layer, gate):
            return w_sb[:, layer, H * (4 + gate):H * (5 + gate)]

        with nc.Block() as block:
            @block.sync
            def _(sp):
                for i, W in enumerate((W0, W1)):
                    sp.dma_start(w_sb[:, i, :], W).then_inc(loaded, 16)
                for i, b in enumerate((b0, b1)):
                    sp.dma_start(b_sb[:, i, :], b).then_inc(loaded, 16)
                sp.wait_ge(emb_zero, 1)
                sp.dma_start(emb_sb[0:TYPES, 1, :], emb).then_inc(loaded, 16)
                sp.dma_start(bm_sb[:, 0, :], bm0.to_broadcast([TC, H])).then_inc(loaded, 16)
                sp.dma_start(bm_sb[:, 1, :], bm1.to_broadcast([TC, H])).then_inc(loaded, 16)
                sp.dma_start(src_sb[:, :], src).then_inc(loaded, 16)
                sp.dma_start(dst_sb[:, :], dst).then_inc(loaded, 16)
                sp.dma_start(typ_sb[:, :], etype).then_inc(loaded, 16)
                sp.dma_start(rows, x).then_inc(loaded, 16)
                sp.wait_ge(loaded, 176)

            @block.gpsimd
            def _(pool):
                pool.memset(emb_sb[:, :, :], 0.0).then_inc(emb_zero, 1)
                pool.iota(iota_i[:, :], [[1, 128]], base=0, channel_multiplier=-1).then_inc(consts, 1)

            @block.vector
            def _(dve):
                dve.memset(zeros[:, :], 0.0)
                dve.wait_ge(consts, 1)
                dve.tensor_copy(ident[:, :], iota_i[:, :]).then_inc(vc, 1)
                dve.wait_ge(vc, 1)
                dve.tensor_scalar(lower[:, :], ident[0:EC, 0:EC], 0.0, None, ALU.is_lt).then_inc(vc, 1)
                dve.wait_ge(vc, 2)
                dve.tensor_scalar(ident[:, :], ident[:, :], 0.0, None, ALU.is_equal).then_inc(vc, 1)
                dve.wait_ge(loaded, 176)
                dve.tensor_copy(typ_f[:, :], typ_sb[:, :]).then_inc(vc, 1)
                dve.wait_ge(vc, 4)
                dve.tensor_scalar(typ_f[:, :], typ_f[:, :], 0.0, float(TYPES - 1), ALU.max, ALU.min).then_inc(vc, 1)
                dve.tensor_tensor(b_sb[:, :, 1:3], b_sb[:, :, 1:3], b_sb[:, :, 4:6], ALU.add).then_inc(vc, 1)
                dve.wait_ge(emb_zero, 1)
                dve.tensor_tensor(emb_sb[:, :, :], emb_sb[:, :, :], bm_sb[:, :, :], ALU.add).then_inc(vc, 1)
                dve.wait_ge(vc, 7)

        iota_ready = sem("iota_ready")
        with nc.Block() as block:
            @block.gpsimd
            def _(pool):
                pool.iota(iota_i[0:EC, 0:TC], [[1, TC]], base=0, channel_multiplier=0).then_inc(iota_ready, 1)

            @block.vector
            def _(dve):
                dve.wait_ge(iota_ready, 1)
                dve.tensor_copy(iota_t[:, :], iota_i[0:EC, 0:TC]).then_inc(vc, 1)
                dve.wait_ge(vc, 8)

        def take(eng, sem, n=1):
            eng.wait_ge(sem, n)
            eng.sem_inc(sem, -n)

        (idx_pool, idx_pe, msg_in, acc_in, scattered, acc_done, idx_used, bcast, same_ready, sel_done,
         zeroed, dve_own) = (sem(n) for n in
            ("idx_pool", "idx_pe", "msg_in", "acc_in", "scattered", "acc_done", "idx_used", "bcast",
             "same_ready", "sel_done", "zeroed", "dve_own"))
        sums_clear = sem("sums_clear")

        def sum_edges(layer, in_sb, out_sb):
            with nc.Block() as block:
                @block.sync
                def _(sp):
                    by_tile = sums.rearrange("(a p) f -> a p f", p=NT)
                    with sp.Fori(0, NTILES // 4) as a:
                        for t in range(4):
                            sp.dma_start(by_tile[a * 4 + t], zeros[:, :]).then_inc(zeroed, 16)
                        take(sp, zeroed, 64)
                    sp.sem_inc(sums_clear, 1)

                @block.gpsimd
                def _(pool):
                    take(pool, sums_clear)
                    with pool.Fori(0, CHUNKS):
                        take(pool, idx_pool, 2)
                        pool.indirect_dma_start(msg_rows[:, :], None, rows,
                                                bass.IndirectOffsetOnAxis(ap=in_row[:, :], axis=0)).then_inc(msg_in, 16)
                        pool.indirect_dma_start(acc[:, :], None, sums,
                                                bass.IndirectOffsetOnAxis(ap=out_row[:, :], axis=0)).then_inc(acc_in, 16)
                        take(pool, acc_done, 2)
                        pool.indirect_dma_start(sums, bass.IndirectOffsetOnAxis(ap=write_row[:, :], axis=0),
                                                acc[:, :], None, bounds_check=NODES - 1, oob_is_err=False).then_inc(scattered, 16)
                        pool.wait_ge(scattered, 16)
                        pool.inc_swdge_sem([msg_in, acc_in, scattered], [16, 16, 16], mode="sub")
                        pool.sem_inc(idx_used, 1)

                @block.vector
                def _(dve):
                    dve.sem_inc(idx_used, 1)
                    with dve.Fori(0, CHUNKS) as c:
                        take(dve, idx_used)
                        dve.tensor_copy(out_f[:, :], out_sb[:, bass.ds(c, 1)]).then_inc(idx_pe, 1)
                        dve.tensor_copy(in_row[:, :], in_sb[:, bass.ds(c, 1)]).then_inc(idx_pool, 1)
                        dve.tensor_copy(out_row[:, :], out_sb[:, bass.ds(c, 1)]).then_inc(idx_pool, 1)
                        if layer:
                            dve.tensor_scalar(msg[:, H:H + TC], iota_t[:, :], typ_f[:, bass.ds(c, 1)], None, ALU.is_equal).then_inc(dve_own, 1)
                        else:
                            dve.tensor_scalar(msg[:, H:H + TC], iota_t[:, :], 0.0, None, ALU.is_equal).then_inc(dve_own, 1)
                        take(dve, bcast)
                        dve.tensor_scalar(same[:, :], banks[0][0:EC, 0:EC], out_f[:, :], None, ALU.is_equal).then_inc(dve_own, 1)
                        dve.wait_ge(dve_own, 2)
                        dve.tensor_tensor(scrap[:, :], same[:, :], lower[:, :], ALU.mult).then_inc(dve_own, 1)
                        dve.wait_ge(dve_own, 3)
                        dve.tensor_reduce(dups[:, :], scrap[:, :], mybir.AxisListType.X, ALU.max).then_inc(dve_own, 1)
                        dve.wait_ge(dve_own, 4)
                        dve.scalar_tensor_tensor(out=write_f[:, :], in0=dups[:, :], scalar=float(FAR), in1=out_f[:, :],
                                                 op0=ALU.mult, op1=ALU.add).then_inc(dve_own, 1)
                        take(dve, dve_own, 5)
                        dve.tensor_copy(write_row[:, :], write_f[:, :]).then_inc(acc_done, 1)
                        dve.wait_ge(msg_in, 16)
                        dve.tensor_copy(msg[:, 0:H], msg_rows[:, :]).then_inc(same_ready, 1)
                        take(dve, sel_done)
                        dve.wait_ge(acc_in, 16)
                        dve.tensor_tensor(acc[:, :], acc[:, :], banks[1][0:EC, 0:H + TC], ALU.add).then_inc(acc_done, 1)
                    take(dve, idx_used)

                @block.tensor
                def _(pe):
                    with pe.Fori(0, CHUNKS):
                        take(pe, idx_pe)
                        pe.transpose(banks[0][0:EC, 0:EC], out_f[:, 0:1].to_broadcast([EC, EC]), ident[0:EC, 0:EC]).then_inc(bcast, 1)
                        take(pe, same_ready)
                        pe.matmul(banks[1][0:EC, 0:H + TC], same[:, :], msg[:, :], start=True, stop=True).then_inc(sel_done, 1)

        (win_in, h_in, res_in, turned, s_done, agg_ps, agg_sb, gates_ps, rz_done, pre_n, n_done, new_done, back_ps,
         var_done, std_done, rows_done, stored) = (sem(n) for n in
            ("win_in", "h_in", "res_in", "turned", "s_done", "agg_ps", "agg_sb", "gates_ps", "rz_done", "pre_n", "n_done",
             "new_done", "back_ps", "var_done", "std_done", "rows_done", "stored"))

        def windows(a):
            return a.rearrange("(w t p) f -> w p t f", t=WT, p=NT)

        def gru(L, residual, result):
            with nc.Block() as block:
                @block.sync
                def _(sp):
                    with sp.Fori(0, WINDOWS) as w:
                        sp.dma_start(s_rows[:, :, :], windows(sums)[w]).then_inc(win_in, 16)
                        sp.dma_start(h_rows[:, :, :], windows(rows)[w]).then_inc(h_in, 16)
                        if residual is not None:
                            sp.dma_start(res[:, :, :], windows(residual)[w]).then_inc(res_in, 16)
                        take(sp, rows_done)
                        sp.dma_start(windows(result)[w], new_rows[:, :, :]).then_inc(stored, 16)
                        take(sp, stored, 16)

                @block.tensor
                def _(pe):
                    with pe.Fori(0, WINDOWS):
                        take(pe, win_in, 16)
                        take(pe, h_in, 16)
                        for t in range(WT):
                            node = slice(t * NT, (t + 1) * NT)
                            pe.transpose(banks[0][:, node], s_rows[:, t, 0:H], ident[0:NT, 0:NT])
                            pe.transpose(banks[1][0:TC, node], s_rows[:, t, H:H + TC], ident[0:NT, 0:NT])
                            mm = pe.transpose(banks[7][:, node], h_rows[:, t, :], ident[0:NT, 0:NT])
                        mm.then_inc(turned, 1)
                        take(pe, s_done)
                        pe.matmul(banks[2][:, 0:WN], w_sb[:, L, 0:H], sT[:, :], start=True, stop=False)
                        pe.matmul(banks[2][:, 0:WN], emb_sb[:, L, :], cT[:, :], start=False, stop=True).then_inc(agg_ps, 1)
                        take(pe, agg_sb)
                        for g in range(2):
                            pe.matmul(banks[3 + g][:, 0:WN], w_ih(L, g), agg[:, :], start=True, stop=False)
                            pe.matmul(banks[3 + g][:, 0:WN], w_hh(L, g), hT[:, :], start=False, stop=True)
                        pe.matmul(banks[5][:, 0:WN], w_ih(L, 2), agg[:, :], start=True, stop=True)
                        pe.matmul(banks[6][:, 0:WN], w_hh(L, 2), hT[:, :], start=True, stop=True).then_inc(gates_ps, 1)
                        take(pe, new_done)
                        for t in range(WT):
                            mm = pe.transpose(banks[0][0:NT, t * H:(t + 1) * H], new_T[:, t * NT:(t + 1) * NT], ident[:, :])
                        mm.then_inc(back_ps, 1)

                @block.scalar
                def _(act):
                    with act.Fori(0, WINDOWS):
                        take(act, gates_ps)
                        act.activation(r_g[:, :], banks[3][:, 0:WN], ACT.Sigmoid, bias=b_sb[:, L, 1:2])
                        act.activation(z_g[:, :], banks[4][:, 0:WN], ACT.Sigmoid, bias=b_sb[:, L, 2:3]).then_inc(rz_done, 1)
                        take(act, pre_n)
                        act.activation(n_g[:, :], t_g[:, :], ACT.Tanh, bias=b_sb[:, L, 3:4]).then_inc(n_done, 1)
                        if residual is not None:
                            take(act, var_done)
                            act.activation(std[:, :], var[:, :], ACT.Sqrt).then_inc(std_done, 1)

                @block.vector
                def _(dve):
                    with dve.Fori(0, WINDOWS):
                        take(dve, turned)
                        dve.tensor_copy(sT[:, :], banks[0][:, 0:WN])
                        dve.tensor_copy(hT[:, :], banks[7][:, 0:WN])
                        dve.tensor_copy(cT[:, :], banks[1][0:TC, 0:WN]).then_inc(s_done, 1)
                        take(dve, agg_ps)
                        dve.tensor_copy(agg[:, :], banks[2][:, 0:WN]).then_inc(agg_sb, 1)
                        take(dve, rz_done)
                        dve.scalar_tensor_tensor(out=t_g[:, :], in0=banks[6][:, 0:WN], scalar=b_sb[:, L, 6:7], in1=r_g[:, :],
                                                 op0=ALU.add, op1=ALU.mult).then_inc(dve_own, 1)
                        take(dve, dve_own)
                        dve.tensor_tensor(t_g[:, :], t_g[:, :], banks[5][:, 0:WN], ALU.add).then_inc(pre_n, 1)
                        take(dve, n_done)
                        dve.tensor_tensor(d_g[:, :], hT[:, :], n_g[:, :], ALU.subtract).then_inc(dve_own, 1)
                        take(dve, dve_own)
                        dve.tensor_tensor(d_g[:, :], d_g[:, :], z_g[:, :], ALU.mult).then_inc(dve_own, 1)
                        take(dve, dve_own)
                        dve.tensor_tensor(new_T[:, :], d_g[:, :], n_g[:, :], ALU.add).then_inc(new_done, 1)
                        take(dve, back_ps)
                        back = banks[0][0:NT, 0:WT * H].rearrange("p (t f) -> p t f", t=WT)
                        if residual is None:
                            dve.tensor_copy(new_rows[:, :, :], back).then_inc(rows_done, 1)
                            return
                        take(dve, res_in, 16)
                        dve.tensor_tensor(res[:, :, :], res[:, :, :], back, ALU.add).then_inc(dve_own, 1)
                        take(dve, dve_own)
                        for t in range(WT):
                            last = dve.bn_stats(stats[:, t, :], res[:, t, :])
                        last.then_inc(dve_own, 1)
                        take(dve, dve_own)
                        for t in range(WT):
                            last = dve.bn_aggr(mv[:, t, :], stats[:, t, :])
                        last.then_inc(dve_own, 1)
                        take(dve, dve_own)
                        dve.tensor_scalar(var[:, :], mv[:, :, 1], EPS, None, ALU.add).then_inc(var_done, 1)
                        take(dve, std_done)
                        dve.reciprocal(rstd[:, :], std[:, :]).then_inc(dve_own, 1)
                        take(dve, dve_own)
                        for t in range(WT):
                            last = dve.tensor_scalar(new_rows[:, t, :], res[:, t, :], mv[:, t, 0:1], rstd[:, t:t + 1],
                                                     ALU.subtract, ALU.mult)
                        last.then_inc(rows_done, 1)

        with nc.Fori(0, STEPS - 1):
            sum_edges(0, dst_sb, src_sb)
            gru(0, None, rows)
        sum_edges(0, dst_sb, src_sb)
        gru(0, x, rows)
        sum_edges(1, src_sb, dst_sb)
        gru(1, rows, out)


P = 128
COLS = 2048
KEYS = P * COLS
ROWS = KEYS // P
RUN = 16
BLOCKS = WINDOWS * NTILES
HALF = BLOCKS // 2
CODE_SHIFT, FROM_SHIFT, TO_SHIFT = 20, 13, 4
PAD_CODE = 2008
JOB_COLS = -(-BLOCKS // P)
EXTRA = JOB_COLS
JC = JOB_COLS + 1
WJ = NTILES + WT
TILE = 512


class Fast:
    pass


def take(eng, sem, n=1):
    eng.wait_ge(sem, n)
    eng.sem_inc(sem, -n)


def find_jobs(nc, f, src, dst, etype):
    with ExitStack() as ctx:
        def sb(name, shape, dt=F32):
            return ctx.enter_context(nc.sbuf_tensor(name, shape, dt))

        def sem(name):
            return ctx.enter_context(nc.semaphore(name))

        banks = [ctx.enter_context(nc.psum_tensor(f"sort_bank{i}", [P, 512], F32)) for i in range(8)]
        bufs = [sb("keys_a", [P, COLS]), sb("keys_b", [P, COLS])]
        making = ExitStack()

        def made(name, dt=F32):
            return making.enter_context(nc.sbuf_tensor(name, [EC, CHUNKS], dt))

        lane = sb("lane", [P, 1], I32)
        bits = sb("bits", [P, 8], I32)
        sign = sb("sign", [P, 9])
        flip = sb("flip", [P, 8])

        raw = [made(n, I32) for n in ("raw_from", "raw_to", "raw_kind")]
        fl = [made(f"fl{i}") for i in range(8)]
        integer, low = made("integer", I32), made("low", I32)

        keys_d = nc.dram_tensor("sorted_keys", [ROWS + 1, P], F32, kind="Internal").ap()
        firsts_d = nc.dram_tensor("first_keys", [ROWS], F32, kind="Internal").ap()

        edges_in, own, sign_ready = sem("edges_in"), sem("own"), sem("sign_ready")
        to_pe, on_psum, off_psum = sem("to_pe"), sem("on_psum"), sem("off_psum")

        own_n = 0
        key_u = bufs[0][:, :].bitcast(U32)

        with nc.Block() as block:
            @block.sync
            def _(sp):
                for t, d in zip(raw, (dst, src, etype)):
                    sp.dma_start(t[:, :], d).then_inc(edges_in, 16)
                sp.wait_ge(edges_in, 48)

            @block.gpsimd
            def _(pool):
                pool.iota(lane[:, :], [[1, 1]], base=0, channel_multiplier=1).then_inc(sign_ready, 1)
                pool.memset(bufs[0][:, :].bitcast(I32), PAD_CODE << CODE_SHIFT).then_inc(sign_ready, 1)

            @block.vector
            def _(dve):
                n = 0

                def step(ins):
                    nonlocal n
                    n += 1
                    ins.then_inc(own, 1)
                    dve.wait_ge(own, n)

                def floor_div(out, x, d):
                    step(dve.tensor_scalar(fl[6][:, :], x, 0.5, 1.0 / d, ALU.add, ALU.mult))
                    step(dve.tensor_copy(integer[:, :], fl[6][:, :]))
                    step(dve.tensor_copy(out, integer[:, :]))
                    step(dve.tensor_tensor(fl[7][:, :], out, fl[6][:, :], ALU.is_gt))
                    step(dve.tensor_tensor(out, out, fl[7][:, :], ALU.subtract))

                frm, to, kind, tile, window, tmp = (t[:, :] for t in fl[0:6])
                dve.wait_ge(edges_in, 48)
                step(dve.tensor_copy(frm, raw[0][:, :]))
                step(dve.tensor_copy(to, raw[1][:, :]))
                step(dve.tensor_copy(kind, raw[2][:, :]))
                step(dve.tensor_scalar(kind, kind, 0.0, float(TYPES - 1), ALU.max, ALU.min))
                floor_div(tile, frm, NT)
                floor_div(window, to, WN)
                step(dve.scalar_tensor_tensor(out=frm, in0=tile, scalar=-float(NT), in1=frm, op0=ALU.mult, op1=ALU.add))
                step(dve.scalar_tensor_tensor(out=to, in0=window, scalar=-float(WN), in1=to, op0=ALU.mult, op1=ALU.add))
                step(dve.scalar_tensor_tensor(out=kind, in0=to, scalar=float(1 << TO_SHIFT), in1=kind, op0=ALU.mult, op1=ALU.add))
                step(dve.scalar_tensor_tensor(out=kind, in0=frm, scalar=float(1 << FROM_SHIFT), in1=kind, op0=ALU.mult, op1=ALU.add))
                step(dve.tensor_copy(low[:, :], kind))
                step(dve.scalar_tensor_tensor(out=tile, in0=window, scalar=-float(WT), in1=tile, op0=ALU.mult, op1=ALU.add))
                step(dve.tensor_scalar(tmp, tile, 0.0, float(NTILES), ALU.is_lt, ALU.mult))
                step(dve.tensor_tensor(tile, tile, tmp, ALU.add))
                step(dve.scalar_tensor_tensor(out=tile, in0=window, scalar=float(NTILES), in1=tile, op0=ALU.mult, op1=ALU.add))
                block_code(dve, step, tile, window, tmp, frm)
                step(dve.tensor_copy(integer[:, :], frm))
                dve.wait_ge(sign_ready, 2)
                step(dve.tensor_scalar(integer[:, :], integer[:, :], CODE_SHIFT, None, ALU.logical_shift_left))
                step(dve.tensor_tensor(bufs[0][0:EC, 0:CHUNKS].bitcast(I32), integer[:, :], low[:, :], ALU.bitwise_or))
                step(dve.memset(sign[:, :], 1.0))
                for b in range(7):
                    step(dve.tensor_scalar(bits[:, b:b + 1], lane[:, :], b, 1, ALU.logical_shift_right, ALU.bitwise_and))
                    step(dve.tensor_scalar(sign[:, b + 1:b + 2], bits[:, b:b + 1], -2.0, 1.0, ALU.mult, ALU.add))
                step(dve.tensor_tensor(flip[:, :], sign[:, 1:9], sign[:, 0:8], ALU.mult))
                dve.sem_inc(own, -n)

        making.close()

        NAT = COLS.bit_length() - 1
        ALL = KEYS.bit_length() - 1
        BANK = 512
        sorted_in = []

        def pairs(buf, j, cols=slice(0, COLS)):
            return buf[:, cols].rearrange("p (a t d) -> p a t d", t=2, d=1 << j)

        with nc.Block() as block:
            @block.vector
            def _(dve):
                n, evicted, cur = 0, 0, 0

                def step(*instructions):
                    nonlocal n
                    n += 1
                    instructions[-1].then_inc(own, 1)
                    dve.wait_ge(own, n)

                for k in range(1, NAT):
                    for j in reversed(range(k)):
                        v, o = (x[:, :].rearrange("p (a r b t d) -> p a r b t d", r=2, b=1 << (k - j - 1), t=2, d=1 << j)
                                for x in (bufs[cur], bufs[1 - cur]))
                        step(*[dve.tensor_tensor(o[:, :, r, :, t, :], v[:, :, r, :, 0, :], v[:, :, r, :, 1, :],
                                                 ALU.min if r == t else ALU.max)
                               for r in range(2) for t in range(2)])
                        cur = 1 - cur
                for k in range(NAT, ALL + 1):
                    flipped = dve.tensor_scalar(bufs[1 - cur][:, :], bufs[cur][:, :], flip[:, k - NAT:k - NAT + 1], None, ALU.mult)
                    cur = 1 - cur
                    if k == NAT:
                        step(flipped)
                    else:
                        flipped.then_inc(to_pe, 4)
                        cur = 1 - cur
                        for j in reversed(range(NAT, k)):
                            first, last = j == k - 1, j == NAT
                            if first or last:
                                for b in range(4):
                                    c = slice(b * BANK, (b + 1) * BANK)
                                    if first:
                                        dve.wait_ge(off_psum, evicted + b + 1)
                                    v, o = pairs(bufs[cur], j - NAT, c), pairs(bufs[1 - cur], j - NAT, c)
                                    dve.tensor_tensor(o[:, :, 0, :], v[:, :, 0, :], v[:, :, 1, :], ALU.min)
                                    ins = dve.tensor_tensor(o[:, :, 1, :], v[:, :, 0, :], v[:, :, 1, :], ALU.max)
                                    if last:
                                        ins.then_inc(to_pe, 1)
                                if not last:
                                    step(ins)
                            else:
                                v, o = pairs(bufs[cur], j - NAT), pairs(bufs[1 - cur], j - NAT)
                                step(dve.tensor_tensor(o[:, :, 0, :], v[:, :, 0, :], v[:, :, 1, :], ALU.min),
                                     dve.tensor_tensor(o[:, :, 1, :], v[:, :, 0, :], v[:, :, 1, :], ALU.max))
                            cur = 1 - cur
                        evicted += 8
                        dve.wait_ge(off_psum, evicted)
                        cur = 1 - cur
                    for j in reversed(range(NAT)):
                        v, o = pairs(bufs[cur], j), pairs(bufs[1 - cur], j)
                        step(dve.tensor_tensor(o[:, :, 0, :], v[:, :, 0, :], v[:, :, 1, :], ALU.min),
                             dve.tensor_tensor(o[:, :, 1, :], v[:, :, 0, :], v[:, :, 1, :], ALU.max))
                        cur = 1 - cur
                sorted_in.append(cur)

            def sources():
                cur = (NAT - 1) * NAT // 2 % 2
                for k in range(NAT, ALL + 1):
                    cur = 1 - cur
                    if k > NAT:
                        yield cur
                        cur = 1 - cur
                        cur = (cur + k - NAT) % 2
                        yield cur
                        cur = 1 - cur
                    cur = (cur + NAT) % 2

            @block.tensor
            def _(pe):
                for turn, cur in enumerate(sources()):
                    for b in range(4):
                        pe.wait_ge(to_pe, turn * 4 + b + 1)
                        for i in range(4 * b, 4 * b + 4):
                            ins = pe.transpose(banks[b][:, (i % 4) * P:(i % 4 + 1) * P], bufs[cur][:, i * P:(i + 1) * P], f.ident[:, :])
                        ins.then_inc(on_psum, 1)

            @block.scalar
            def _(act):
                for turn, cur in enumerate(sources()):
                    for b in range(4):
                        act.wait_ge(on_psum, turn * 4 + b + 1)
                        act.copy(bufs[1 - cur][:, b * BANK:(b + 1) * BANK], banks[b][:, :]).then_inc(off_psum, 1)

        f.keys, f.spare = bufs[sorted_in[0]], bufs[1 - sorted_in[0]]
        f.keys_d, f.firsts_d = keys_d, firsts_d
        cut_jobs(nc, f, sem, sb, banks)


def block_code(dve, step, number, neg, tmp, out):
    step(dve.tensor_scalar(neg, number, float(HALF), None, ALU.is_lt))
    step(dve.tensor_scalar(tmp, number, -1.0, float(HALF - 1), ALU.mult, ALU.add))
    step(dve.tensor_scalar(number, number, -float(HALF), None, ALU.add))
    step(dve.tensor_tensor(out, number, tmp, ALU.max))
    step(dve.scalar_tensor_tensor(out=out, in0=neg, scalar=2048.0, in1=out, op0=ALU.mult, op1=ALU.add))
    step(dve.tensor_scalar(out, out, 8.0, None, ALU.add))


def cut_jobs(nc, f, sem, sb, banks):
    firsts = sb("firsts", [P, ROWS])
    shifted = sb("shifted", [P, COLS])
    scrap = sb("scrap_n", [P, COLS])
    number = sb("number", [P, JC])
    number_i = sb("number_i", [P, JC], I32)
    t1, t2, code, rounded = (sb(n, [P, JC]) for n in ("t1", "t2", "code", "rounded"))
    code_i, low_i, rows_i = sb("code_i", [P, JC], I32), sb("low_i", [P, JC], I32), sb("rows_i", [P, 2, JC + 1], U32)
    lo = sb("lo", [P, JC])
    passed = sb("passed", [P, JC])
    start = sb("start", [P, JC])
    row_a = sb("row_a", [P, JC + 1, P])
    row_b = sb("row_b", [P, JC, P])
    field = sb("field", [P, JC, P])
    field_i = sb("field_i", [P, JC, P], I32)
    mask = sb("mask", [P, JC, P], I32)
    match = sb("match", [P, JC, P])
    lanes = sb("lanes", [P, P])
    sums = sb("sums", [P, 2])
    bad = sb("bad", [1, 2])
    stored, firsts_in, shifted_in = sem("stored_keys"), sem("firsts_in"), sem("shifted_in")
    iota_in, rows_ready, rows_in, rows2_in = sem("iota_in"), sem("rows_ready"), sem("rows_in"), sem("rows2_in")
    own, fields, turned, moved, total = sem("own2"), sem("fields"), sem("turned2"), sem("moved"), sem("total")
    field_used = sem("field_used")
    n_pads = KEYS - EDGES

    with nc.Block() as block:
        @block.sync
        def _(sp):
            with nc.allow_non_contiguous_dma(reason="one key of each row"):
                sp.dma_start(f.firsts_d.rearrange("(p a) -> p a", p=P), f.keys[:, 0:COLS:P]).then_inc(stored, 16)
            sp.dma_start(f.keys_d[0:ROWS].rearrange("(p a) b -> p (a b)", p=P), f.keys[:, :]).then_inc(stored, 16)
            sp.dma_start(f.keys_d[ROWS:ROWS + 1, :], f.zeros[0:1, 0:P]).then_inc(stored, 16)
            sp.wait_ge(stored, 48)
            sp.dma_start(firsts[:, :], f.firsts_d.rearrange("(a b) -> a b", a=1).to_broadcast([P, ROWS])).then_inc(firsts_in, 16)
            flat = f.keys_d.rearrange("a b -> (a b)")
            sp.dma_start(shifted[:, :], flat[RUN:RUN + KEYS].rearrange("(p c) -> p c", p=P)).then_inc(shifted_in, 16)
            sp.wait_ge(shifted_in, 16)

        @block.gpsimd
        def _(pool):
            pool.iota(number_i[:, 0:EXTRA], [[P, JOB_COLS]], base=0, channel_multiplier=1)
            pool.iota(number_i[:, EXTRA:JC], [[0, 1]], base=0, channel_multiplier=1).then_inc(iota_in, 1)
            pool.wait_ge(iota_in, 1)
            pool.iota(field_i[:, 0, :], [[1, P]], base=0, channel_multiplier=0).then_inc(iota_in, 1)
            pool.wait_ge(rows_ready, 1)
            pool.wait_ge(stored, 48)

            def gather(out, index, sem_in):
                pool.indirect_dma_start(out, None, f.keys_d, bass.IndirectOffsetOnAxis(ap=index, axis=0)).then_inc(sem_in, 16)

            for c in range(JC):
                gather(row_a[:, c, :], rows_i[:, 0, c:c + 1], rows_in)
            gather(row_a[:, JC, :], rows_i[:, 1, EXTRA:JC], rows2_in)
            for c in range(JC):
                gather(row_b[:, c, :], rows_i[:, 1, c:c + 1] if c < EXTRA else rows_i[:, 1, JC:JC + 1], rows2_in)

        @block.vector
        def _(dve):
            n = 0

            def step(ins):
                nonlocal n
                n += 1
                ins.then_inc(own, 1)
                dve.wait_ge(own, n)

            def bc(x, cols=JC):
                return x[:, 0:cols].unsqueeze(2).to_broadcast([P, cols, P])

            dve.wait_ge(iota_in, 2)
            step(dve.tensor_copy(number[:, :], number_i[:, :]))
            step(dve.tensor_copy(lanes[:, :], field_i[:, 0, :]))
            e = slice(EXTRA, JC)
            step(dve.tensor_scalar(t1[:, e], number[:, e], 0.5, 1.0 / WT, ALU.add, ALU.mult))
            step(dve.tensor_copy(code_i[:, e], t1[:, e]))
            step(dve.tensor_copy(rounded[:, e], code_i[:, e]))
            step(dve.tensor_tensor(t2[:, e], rounded[:, e], t1[:, e], ALU.is_gt))
            step(dve.tensor_tensor(rounded[:, e], rounded[:, e], t2[:, e], ALU.subtract))
            step(dve.scalar_tensor_tensor(out=number[:, e], in0=rounded[:, e], scalar=float(NTILES - WT), in1=number[:, e],
                                          op0=ALU.mult, op1=ALU.add))
            block_code(dve, step, number[:, :], t1[:, :], t2[:, :], code[:, :])
            step(dve.tensor_copy(code_i[:, :], code[:, :]))
            step(dve.tensor_scalar(t1[:, :], t1[:, :], float((1 << CODE_SHIFT) - 1), None, ALU.mult))
            step(dve.tensor_copy(low_i[:, :], t1[:, :]))
            step(dve.tensor_scalar(code_i[:, :], code_i[:, :], CODE_SHIFT, None, ALU.logical_shift_left))
            step(dve.tensor_tensor(lo[:, :].bitcast(I32), code_i[:, :], low_i[:, :], ALU.bitwise_or))
            dve.wait_ge(firsts_in, 16)
            for c in range(JC):
                step(dve.tensor_scalar(scrap[:, :], firsts[:, :], lo[:, c:c + 1], None, ALU.is_lt, ALU.add,
                                       accum_out=passed[:, c:c + 1]))
            step(dve.tensor_scalar(t1[:, :], passed[:, :], -1.0, 0.0, ALU.add, ALU.max))
            step(dve.tensor_copy(rows_i[:, 0, 0:JC], t1[:, :]))
            step(dve.tensor_scalar(t2[:, :], t1[:, :], 1.0, float(ROWS - 1), ALU.add, ALU.min))
            step(dve.tensor_copy(rows_i[:, 1, 0:JC], t2[:, :]))
            step(dve.tensor_scalar(t2[:, e], t1[:, e], 2.0, float(ROWS - 1), ALU.add, ALU.min))
            step(dve.tensor_copy(rows_i[:, 1, JC:JC + 1], t2[:, e]))
            dve.sem_inc(rows_ready, 1)

            a, b = f.keys[:, :].bitcast(I32), shifted[:, :].bitcast(I32)
            dve.wait_ge(shifted_in, 16)
            step(dve.tensor_scalar(f.spare[:, :].bitcast(I32), a, FROM_SHIFT, None, ALU.logical_shift_right))
            step(dve.tensor_scalar(b, b, FROM_SHIFT, None, ALU.logical_shift_right))
            step(dve.tensor_tensor(scrap[:, :], f.spare[:, :].bitcast(I32), b, ALU.is_equal))
            step(dve.tensor_reduce(sums[:, 1:2], scrap[:, :], AX.X, ALU.add))

            dve.wait_ge(rows_in, 16 * JC)
            step(dve.tensor_tensor(field[:, :, :], row_a[:, 0:JC, :], bc(lo), ALU.is_lt))
            step(dve.tensor_reduce(start[:, :], field[:, :, :], AX.X, ALU.add))
            step(dve.tensor_tensor(mask[:, :, :], lanes[:, :].unsqueeze(1).to_broadcast([P, JC, P]), bc(start), ALU.is_ge))
            dve.wait_ge(rows2_in, 16 * (JC + 1))
            step(dve.tensor_copy(row_a[:, EXTRA, :], row_a[:, JC, :]))
            step(dve.copy_predicated(row_b[:, :, :], mask[:, :, :], row_a[:, 0:JC, :]))
            key = row_b[:, :, :].bitcast(I32)
            step(dve.tensor_scalar(field_i[:, :, :], key, CODE_SHIFT, (1 << 12) - 1, ALU.logical_shift_right, ALU.bitwise_and))
            step(dve.tensor_tensor(match[:, :, :], field_i[:, :, :], bc(code), ALU.is_equal))
            step(dve.tensor_reduce(sums[:, 0:1], match[:, :, :], AX.XY, ALU.add))
            step(dve.tensor_scalar(field_i[:, :, :], key, FROM_SHIFT, 127, ALU.logical_shift_right, ALU.bitwise_and))
            step(dve.scalar_tensor_tensor(out=field[:, :, :], in0=field_i[:, :, :], scalar=1.0, in1=match[:, :, :],
                                          op0=ALU.add, op1=ALU.mult))
            dve.sem_inc(fields, 1)
            dve.wait_ge(field_used, 1)
            step(dve.tensor_scalar(field_i[:, :, :], key, TO_SHIFT, 511, ALU.logical_shift_right, ALU.bitwise_and))
            step(dve.tensor_copy(field[:, :, :], field_i[:, :, :]))
            dve.sem_inc(fields, 1)
            dve.wait_ge(field_used, 2)
            step(dve.tensor_scalar(field_i[:, :, :], key, 15, None, ALU.bitwise_and))
            step(dve.tensor_copy(field[:, :, :], field_i[:, :, :]))
            dve.sem_inc(fields, 1)
            dve.wait_ge(total, 1)
            step(dve.tensor_scalar(bad[:, 0:1], banks[7][0:1, 0:1], float(EDGES), None, ALU.not_equal))
            step(dve.tensor_scalar(bad[:, 1:2], banks[7][0:1, 1:2], float(n_pads - RUN), None, ALU.not_equal))
            step(dve.tensor_tensor(f.general[:, :], bad[:, 0:1], bad[:, 1:2], ALU.max))

        @block.tensor
        def _(pe):
            m = 0
            for i in range(3):
                pe.wait_ge(fields, i + 1)
                for c0 in range(0, JC, 4):
                    if m >= 7:
                        pe.wait_ge(moved, m - 6)
                    for c in range(c0, min(c0 + 4, JC)):
                        ins = pe.transpose(banks[m % 7][:, (c - c0) * P:(c - c0 + 1) * P], field[:, c, :], f.ident[:, :])
                    ins.then_inc(turned, 1)
                    m += 1
            pe.matmul(banks[7][0:1, 0:2], f.ones[:, 0:1], sums[:, :], start=True, stop=True).then_inc(total, 1)

        @block.scalar
        def _(act):
            m = 0
            for i, out in enumerate((f.job_from, f.job_to, f.job_kind)):
                for c0 in range(0, JC, 4):
                    width = (min(c0 + 4, JC) - c0) * P
                    act.wait_ge(turned, m + 1)
                    act.activation(out[:, c0 * P:c0 * P + width], banks[m % 7][:, 0:width], ACT.Copy,
                                   bias=-1.0 if i == 0 else 0.0).then_inc(moved, 1)
                    m += 1
                    if m % -(-JC // 4) == 0:
                        act.wait_ge(moved, m)
                        act.sem_inc(field_used, 1)


GROUP = WT
GROUPS = NTILES // GROUP
LOAD = 10
LOADS = NTILES // LOAD
SLOTS = 5
BATCH = 8
WORDS = TILE // 4


def build(nc, f):
    with ExitStack() as ctx:
        def sb(name, shape, dt=F32):
            return ctx.enter_context(nc.sbuf_tensor(name, shape, dt))

        def sem(name):
            return ctx.enter_context(nc.semaphore(name))

        pair = [ctx.enter_context(nc.psum_tensor(f"tile_pair{i}", [P, 2, TILE], F32)) for i in range(2)]
        col_i = sb("col_i", [P, TILE], I32)
        col = sb("col", [P, TILE], F16)
        col_b = sb("col_b", [P, P, BATCH], F16)
        from_w, to_w, kind_w = (sb(n, [P, WJ], F16) for n in ("from_w", "to_w", "kind_w"))
        to_f = sb("to_f", [P, WJ])
        hot_from = [sb(f"hot_from{i}", [P, P, BATCH], F16) for i in range(3)]
        hot_kind = [sb(f"hot_kind{i}", [P, BATCH, TC], F16) for i in range(3)]
        hot_to = [sb(f"hot_to{i}", [P, WN], F16) for i in range(BATCH)]
        strip = [sb(f"strip{i}", [P, GROUP * WORDS], U32) for i in range(SLOTS)]

        iota_in, col_ready, own = sem("build_iota"), sem("col_ready"), sem("build_own")
        hot_ready, hot_free = sem("hot_ready"), sem("hot_free")
        pair_ready, pair_free = sem("pair_ready"), [sem("pair_free0"), sem("pair_free1")]
        strip_ready, strip_free = sem("strip_ready"), sem("strip_free")
        strip_out = [sem(f"strip_out{i}") for i in range(SLOTS)]

        jobs = [(i, c) for i in range(WT) for c in (i, WT + i)] + [(i, WT + i) for i in range(WT, NTILES)]
        batches = WJ // BATCH
        ring = [b % 2 for b in range(batches - 1)] + [2]

        with nc.Block() as block:
            @block.gpsimd
            def _(pool):
                pool.iota(col_i[:, :], [[1, TILE]], base=0, channel_multiplier=0).then_inc(iota_in, 1)

            @block.vector
            def _(dve):
                take(dve, iota_in)
                dve.tensor_copy(col[:, :], col_i[:, :])
                dve.tensor_copy(col_b[:, :, :], col_i[:, 0:P].unsqueeze(2).to_broadcast([P, P, BATCH])).then_inc(own, 1)
                take(dve, own)
                dve.sem_inc(hot_free, BATCH - 1)
                with dve.Fori(0, WINDOWS) as w:
                    dve.drain()
                    for out, jobs_of in ((from_w, f.job_from), (kind_w, f.job_kind), (to_f, f.job_to)):
                        dve.tensor_copy(out[:, 0:WT], jobs_of[:, bass.ds(w * WT + EXTRA * P, WT)])
                        last = dve.tensor_copy(out[:, WT:WJ], jobs_of[:, bass.ds(w * NTILES, NTILES)])
                    last.then_inc(own, 1)
                    take(dve, own)
                    for n, (_, c) in enumerate(jobs):
                        b, i = divmod(n, BATCH)
                        if i == 0:
                            cols = slice(b * BATCH, (b + 1) * BATCH)
                            dve.tensor_tensor(hot_from[ring[b]][:, :, :], col_b[:, :, :],
                                              from_w[:, cols].unsqueeze(1).to_broadcast([P, P, BATCH]), ALU.is_equal)
                            dve.tensor_tensor(hot_kind[ring[b]][:, :, :], col[:, 0:TC].unsqueeze(1).to_broadcast([P, BATCH, TC]),
                                              kind_w[:, cols].unsqueeze(2).to_broadcast([P, BATCH, TC]), ALU.is_equal)
                        take(dve, hot_free)
                        dve.tensor_scalar(hot_to[i][:, :], col[:, 0:WN], to_f[:, c:c + 1], None, ALU.is_equal).then_inc(hot_ready, 1)
                take(dve, hot_free, BATCH - 1)

            @block.tensor
            def _(pe):
                with pe.Fori(0, WINDOWS):
                    for n, (slot, c) in enumerate(jobs):
                        b, i = divmod(c, BATCH)
                        half = slot // 2 % 2
                        out = pair[half][:, slot % 2, :]
                        start = n == 0 or jobs[n - 1][0] != slot
                        stop = n == WJ - 1 or jobs[n + 1][0] != slot
                        if start and slot % 2 == 0:
                            take(pe, pair_free[half])
                        take(pe, hot_ready)
                        lhs = hot_from[ring[b]][:, :, i]
                        pe.matmul(out[:, WN:TILE], lhs, hot_kind[ring[b]][:, i, :], start=start, stop=stop,
                                  skip_group_check=True).then_inc(hot_free, 1)
                        ins = pe.matmul(out[:, 0:WN], lhs, hot_to[n % BATCH][:, :], start=False, stop=stop, skip_group_check=True)
                        if stop and slot % 2 == 1:
                            ins.then_inc(pair_ready, 1)

            @block.scalar
            def _(act):
                act.sem_inc(pair_free[0], 1)
                act.sem_inc(strip_free, SLOTS)
                with act.Fori(0, WINDOWS):
                    for g in range(GROUPS):
                        take(act, strip_free)
                        for half in range(2):
                            take(act, pair_ready)
                            words = strip[g % SLOTS][:, 2 * half * WORDS:2 * (half + 1) * WORDS]
                            act.activation(words.bitcast(F8), pair[half][:, :, :].rearrange("p a b -> p (a b)"), ACT.Copy,
                                           saturate=False).then_inc(strip_ready if half else pair_free[0], 1)
                take(act, strip_free, SLOTS)

            @block.sync
            def _(sp):
                sp.sem_inc(pair_free[1], 1)
                with sp.Fori(0, WINDOWS) as w:
                    def sent(g):
                        take(sp, strip_out[g % SLOTS], 16)
                        sp.sem_inc(strip_free, 1)

                    for g in range(GROUPS):
                        take(sp, strip_ready)
                        sp.sem_inc(pair_free[1], 1)
                        at = (w + g) % GROUPS * (GROUP * WORDS)
                        sp.dma_start(f.tiles_d[w][:, bass.ds(at, GROUP * WORDS)], strip[g % SLOTS][:, :]).then_inc(strip_out[g % SLOTS], 16)
                        if g >= SLOTS - 2:
                            sent(g - SLOTS + 2)
                    for g in range(GROUPS - SLOTS + 2, GROUPS):
                        sent(g)

        with nc.Block() as block:
            @block.tensor
            def _(pe):
                take(pe, pair_free[0])
                take(pe, pair_free[1])


def windows_of(a):
    return a.rearrange("(w t p) f -> w p t f", t=WT, p=NT)


LOW = 2048.0


def network(nc, f, x, xT, out):
    with ExitStack() as ctx:
        def sb(name, shape, dt=F32):
            return ctx.enter_context(nc.sbuf_tensor(name, shape, dt))

        def sem(name):
            return ctx.enter_context(nc.semaphore("net_" + name))

        banks = [ctx.enter_context(nc.psum_tensor(f"net_bank{i}", [P, TILE], F32)) for i in range(8)]
        high_ps, low_ps, gates_ps = banks[0], banks[1], banks[2:6]
        msg_ps, turn_ps = banks[6], banks[7]

        msgs = [sb(f"messages{i}", [P, NTILES, 2, H], F16) for i in range(2)]
        h, agg, high = sb("h_win", [H, WN]), sb("agg_win", [H, WN]), sb("high_win", [H, WN])
        r_g, z_g, n_g, t_g, d_g, new = (sb(n + "_win", [H, WN]) for n in ("r", "z", "n", "t", "d", "new"))
        msg, rest = sb("msg_win", [NT, WT, H]), sb("rest_win", [NT, WT, H])
        res, rows = sb("res_win", [NT, WT, H]), sb("rows_win", [NT, WT, H])
        stats, mv = sb("stats_win", [NT, WT, 6]), sb("mv_win", [NT, WT, 2])
        var, std, rstd = (sb(n + "_win", [NT, WT]) for n in ("var", "std", "rstd"))

        (h_in, res_in, sums_done, high_out, agg_ready, gates_done, rz_ready, pre_n, n_ready, new_ready, back_done,
         var_ready, std_ready, rows_ready, yT_done, yT_ready, msg_done, msg_ready, high_ready, rest_ready, state_out,
         rows_out, own, load_free) = (sem(n) for n in
            ("h_in", "res_in", "sums_done", "high_out", "agg_ready", "gates_done", "rz_ready", "pre_n", "n_ready", "new_ready",
             "back_done", "var_ready", "std_ready", "rows_ready", "yT_done", "yT_ready", "msg_done", "msg_ready", "high_ready",
             "rest_ready", "state_out", "rows_out", "own", "load_free"))
        load_in = [sem(f"load_in{i}") for i in range(SLOTS)]

        state_d = nc.dram_tensor("state_T", [H, NODES], F32, kind="Internal").ap()
        rows_d = nc.dram_tensor("normed_rows", [NODES, H], F32, kind="Internal").ap()

        def window(a, w):
            return a[:, bass.ds(w * WN, WN)]

        def pe_messages(pe, Lm, of):
            for t in range(WT):
                ins = pe.matmul(msg_ps[0:NT, t * H:(t + 1) * H], of[:, t * NT:(t + 1) * NT], f.w[:, Lm, 0:H], start=True, stop=True)
            ins.then_inc(msg_done, 1)

        def by_tile(ps):
            return ps[0:NT, :].rearrange("p (t f) -> p t f", t=WT)

        def dve_messages(dve, Lm, to, w):
            take(dve, msg_done)
            dve.drain()
            dve.tensor_tensor(msg[:, :, :], by_tile(msg_ps), f.b_msg[0:NT, Lm, :].unsqueeze(1).to_broadcast([NT, WT, H]), ALU.add).then_inc(msg_ready, 1)
            take(dve, high_ready)
            dve.tensor_tensor(rest[:, :, :], msg[:, :, :], to[0:NT, bass.ds(w * WT, WT), 0, :], ALU.subtract).then_inc(rest_ready, 1)

        def act_messages(act, to, w, then=None):
            take(act, msg_ready)
            act.copy(to[0:NT, bass.ds(w * WT, WT), 0, :], msg[:, :, :]).then_inc(high_ready, 1)
            if then:
                then()
            take(act, rest_ready)
            act.activation(to[0:NT, bass.ds(w * WT, WT), 1, :], rest[:, :, :], ACT.Copy, scale=LOW)

        def pe_gates(pe, L):
            take(pe, h_in, 16)
            for g in range(2):
                pe.matmul(gates_ps[g][:, 0:WN], f.w_ih(L, g), agg[:, :], start=True, stop=False)
                pe.matmul(gates_ps[g][:, 0:WN], f.w_hh(L, g), h[:, :], start=False, stop=True)
            pe.matmul(gates_ps[2][:, 0:WN], f.w_ih(L, 2), agg[:, :], start=True, stop=True)
            pe.matmul(gates_ps[3][:, 0:WN], f.w_hh(L, 2), h[:, :], start=True, stop=True).then_inc(gates_done, 1)

        def act_gates(act, L):
            take(act, gates_done)
            act.activation(r_g[:, :], gates_ps[0][:, 0:WN], ACT.Sigmoid, bias=f.b[:, L, 1:2])
            act.activation(z_g[:, :], gates_ps[1][:, 0:WN], ACT.Sigmoid, bias=f.b[:, L, 2:3]).then_inc(rz_ready, 1)
            take(act, pre_n)
            act.activation(n_g[:, :], t_g[:, :], ACT.Tanh, bias=f.b[:, L, 3:4]).then_inc(n_ready, 1)

        def dve_gates(dve, L):
            take(dve, rz_ready)
            dve.scalar_tensor_tensor(out=d_g[:, :], in0=gates_ps[3][:, 0:WN], scalar=f.b[:, L, 6:7], in1=r_g[:, :],
                                     op0=ALU.add, op1=ALU.mult).then_inc(own, 1)
            take(dve, own)
            dve.tensor_tensor(t_g[:, :], d_g[:, :], gates_ps[2][:, 0:WN], ALU.add).then_inc(pre_n, 1)
            take(dve, n_ready)
            dve.tensor_tensor(d_g[:, :], h[:, :], n_g[:, :], ALU.subtract).then_inc(own, 1)
            take(dve, own)
            dve.tensor_tensor(t_g[:, :], d_g[:, :], z_g[:, :], ALU.mult).then_inc(own, 1)
            take(dve, own)
            dve.tensor_tensor(new[:, :], t_g[:, :], n_g[:, :], ALU.add).then_inc(new_ready, 1)

        def pe_back(pe, bank):
            take(pe, new_ready)
            for t in range(WT):
                ins = pe.transpose(bank[0:NT, t * H:(t + 1) * H], new[:, t * NT:(t + 1) * NT], f.ident[:, :])
            ins.then_inc(back_done, 1)

        def dve_norm(dve, bank):
            take(dve, back_done)
            take(dve, res_in, 16)
            dve.tensor_tensor(msg[:, :, :], res[:, :, :], by_tile(bank), ALU.add).then_inc(own, 1)
            take(dve, own)
            for t in range(WT):
                last = dve.bn_stats(stats[:, t, :], msg[:, t, :])
            last.then_inc(own, 1)
            take(dve, own)
            for t in range(WT):
                last = dve.bn_aggr(mv[:, t, :], stats[:, t, :])
            last.then_inc(own, 1)
            take(dve, own)
            dve.tensor_scalar(var[:, :], mv[:, :, 1], EPS, None, ALU.add).then_inc(var_ready, 1)
            take(dve, std_ready)
            dve.reciprocal(rstd[:, :], std[:, :]).then_inc(own, 1)
            take(dve, own)
            for t in range(WT):
                last = dve.tensor_scalar(rows[:, t, :], msg[:, t, :], mv[:, t, 0:1], rstd[:, t:t + 1], ALU.subtract, ALU.mult)
            return last

        def act_norm(act):
            take(act, var_ready)
            act.activation(std[:, :], var[:, :], ACT.Sqrt).then_inc(std_ready, 1)

        def act_sums(act):
            take(act, sums_done)
            act.copy(high[:, :], high_ps[:, 0:WN]).then_inc(high_out, 1)

        def dve_sums(dve):
            take(dve, high_out)
            dve.scalar_tensor_tensor(out=agg[:, :], in0=low_ps[:, 0:WN], scalar=1.0 / LOW, in1=high[:, :],
                                     op0=ALU.mult, op1=ALU.add).then_inc(agg_ready, 1)

        def first_messages():
            with nc.Block() as block:
                @block.sync
                def _(sp):
                    sp.dma_start(state_d, xT).then_inc(state_out, 16)
                    with sp.Fori(0, WINDOWS) as w:
                        take(sp, state_free)
                        sp.dma_start(h[:, :], window(xT, w)).then_inc(h_in, 16)

                @block.tensor
                def _(pe):
                    with pe.Fori(0, WINDOWS):
                        take(pe, h_in, 16)
                        pe_messages(pe, 0, h)

                @block.vector
                def _(dve):
                    dve.sem_inc(state_free, 1)
                    with dve.Fori(0, WINDOWS) as w:
                        dve_messages(dve, 0, msgs[0], w)
                        dve.sem_inc(state_free, 1)

                @block.scalar
                def _(act):
                    with act.Fori(0, WINDOWS) as w:
                        act_messages(act, msgs[0], w)

            with nc.Block() as block:
                @block.sync
                def _(sp):
                    take(sp, state_free)
                    take(sp, state_out, 16)

        state_free = sem("state_free")

        def advance(now, after_it, norm):
            Lm = 1 if norm else 0

            with nc.Block() as block:
                @block.sync
                def _(sp):
                    with sp.Fori(0, WINDOWS) as w:
                        for g in range(LOADS):
                            take(sp, load_free)
                            sp.dma_start(loads[g % SLOTS][:, :], f.tiles_d[w][:, g * LOAD * WORDS:(g + 1) * LOAD * WORDS]).then_inc(load_in[g % SLOTS], 16)
                    take(sp, load_free, SLOTS)

                @block.tensor
                def _(pe):
                    def sums(first, post):
                        if not first:
                            take(pe, agg_ready)
                            pe.sem_inc(load_free, 1)
                        for g in range(LOADS):
                            take(pe, load_in[g % SLOTS], 16)
                            for i in range(LOAD):
                                k = g * LOAD + i
                                counts = loads[g % SLOTS][0:NT, i * WORDS:(i + 1) * WORDS].bitcast(F8)[:, 0:WN]
                                for half, ps in enumerate((high_ps, low_ps)):
                                    ins = pe.matmul(ps[:, 0:WN], msgs[now][0:NT, k, half, :], counts, start=k == 0, stop=k == NTILES - 1)
                            ins.then_inc(*((load_free, 1) if g < LOADS - 1 else (sums_done, 1)))
                            if post:
                                after(g)

                    def after(g):
                        if g == 1:
                            pe_gates(pe, 0)
                        if norm:
                            if g == 3:
                                pe_back(pe, turn_ps)
                            if g == 6:
                                take(pe, rows_ready)
                                for t in range(WT):
                                    ins = pe.transpose(turn_ps[:, t * NT:(t + 1) * NT], rows[:, t, :], f.ident[0:NT, 0:NT])
                                ins.then_inc(yT_done, 1)
                            if g == LOADS - 1:
                                take(pe, yT_ready)
                                pe_messages(pe, Lm, new)
                        elif g == LOADS - 1:
                            take(pe, new_ready)
                            pe_messages(pe, Lm, new)

                    pe.sem_inc(load_free, SLOTS)
                    sums(True, False)
                    with pe.Fori(1, WINDOWS):
                        sums(False, True)
                    take(pe, agg_ready)
                    pe.sem_inc(load_free, 1)
                    for g in range(LOADS):
                        after(g)

                @block.scalar
                def _(act):
                    def load_state(w):
                        act.dma_start(h[:, :], window(state_d, w)).then_inc(h_in, 16)
                        if norm:
                            act.dma_start(res[:, :, :], windows_of(x)[w]).then_inc(res_in, 16)

                    def post(w, last):
                        def move():
                            act.dma_start(window(state_d, w), new[:, :]).then_inc(state_out, 16)
                            if norm:
                                act.dma_start(windows_of(rows_d)[w], rows[:, :, :]).then_inc(rows_out, 16)
                            if not last:
                                load_state(w + 1)

                        act_gates(act, 0)
                        if norm:
                            act_norm(act)
                        act_messages(act, msgs[after_it], w, move)

                    load_state(0)
                    act_sums(act)
                    with act.Fori(1, WINDOWS) as w:
                        post(w - 1, False)
                        act_sums(act)
                    post(WINDOWS - 1, True)

                @block.vector
                def _(dve):
                    def post(w):
                        dve.drain()
                        dve_gates(dve, 0)
                        if norm:
                            dve_norm(dve, turn_ps).then_inc(rows_ready, 1)
                            take(dve, yT_done)
                            dve.tensor_copy(new[:, :], turn_ps[:, 0:WN]).then_inc(yT_ready, 1)
                        dve_messages(dve, Lm, msgs[after_it], w)
                        take(dve, state_out, 16)
                        if norm:
                            take(dve, rows_out, 16)

                    dve_sums(dve)
                    with dve.Fori(1, WINDOWS) as w:
                        post(w - 1)
                        dve_sums(dve)
                    post(WINDOWS - 1)

        with ExitStack() as ring:
            loads = [ring.enter_context(nc.sbuf_tensor(f"load{i}", [P, LOAD * WORDS], U32)) for i in range(SLOTS)]
            first_messages()
            with nc.Fori(0, STEPS // 2):
                advance(0, 1, False)
                advance(1, 0, False)
            advance(0, 1, True)

        PART = WINDOWS // SLOTS
        KINDS_TURN, EMBED, GATES, BACK, STORE = 10, 20, 30, 60, 84
        strips = [sb(f"strips{i}", [P, PART, GROUP, WORDS], U32) for i in range(SLOTS)]
        turned = [sb(f"turned{i}", [NT, WN], F16) for i in range(4)]
        ident16 = sb("ident16", [NT, NT], F16)
        kinds = sb("kinds", [NT, WINDOWS, GROUP, TC])
        kind_sums, kindT = sb("kind_sums", [NT, GROUP, TC]), sb("kindT", [TC, WN])
        agg_msgs = sb("agg_msgs", [H, WN])
        tile_done, tile_out = [sem("tile_done_act"), sem("tile_done_dve")], [sem("tile_out_act"), sem("tile_out_dve")]
        ident_ready = sem("ident_ready")
        kinds_ready, kindT_done, kindT_ready, embed_done, agg_full = (
            sem(n) for n in ("kinds_ready", "kindT_done", "kindT_ready", "embed_done", "agg_full"))
        turn = banks[6:8]
        L = 1

        with nc.Block() as block:
            @block.sync
            def _(sp):
                by_node = f.tiles_d.rearrange("w p c -> p w c")
                with sp.Fori(0, WINDOWS) as v:
                    for i in range(SLOTS):
                        take(sp, load_free)
                        sp.dma_start(strips[i][:, :, :, :].rearrange("p w g c -> p w (g c)"),
                                     by_node[:, i * PART:(i + 1) * PART, bass.ds(v * GROUP * WORDS, GROUP * WORDS)]).then_inc(load_in[i], 16)
                take(sp, load_free, SLOTS)

            @block.tensor
            def _(pe):
                def transpose_tile(k):
                    w, a = divmod(k, WT)
                    if k % (PART * WT) == 0:
                        take(pe, load_in[w // PART], 16)
                    if k >= 2:
                        take(pe, tile_out[k % 2])
                    for g in range(GROUP):
                        counts = strips[w // PART][0:NT, w % PART, g, :].bitcast(F8)[:, a * NT:(a + 1) * NT]
                        ins = pe.matmul(turn[k % 2][0:NT, g * NT:(g + 1) * NT], counts, ident16[:, :], start=True, stop=True)
                    ins.then_inc(tile_done[k % 2], 1)

                def products(k):
                    for half, ps in enumerate((high_ps, low_ps)):
                        ins = pe.matmul(ps[:, 0:WN], msgs[1][0:NT, k, half, :], turned[k % 4][:, :], start=k == 0, stop=k == NTILES - 1)
                    return ins

                def after(k):
                    if k == KINDS_TURN:
                        take(pe, kinds_ready)
                        for g in range(GROUP):
                            ins = pe.transpose(gates_ps[0][0:TC, g * NT:(g + 1) * NT], kind_sums[:, g, :], f.ident[0:NT, 0:NT])
                        ins.then_inc(kindT_done, 1)
                    if k == EMBED:
                        take(pe, kindT_ready)
                        pe.matmul(gates_ps[1][:, 0:WN], f.emb[:, :], kindT[:, :], start=True, stop=True).then_inc(embed_done, 1)
                    if k == GATES:
                        take(pe, agg_full)
                        pe_gates(pe, L)
                    if k == BACK:
                        pe_back(pe, gates_ps[0])

                def window_sums(first):
                    if not first:
                        take(pe, agg_ready)
                    for k in range(NTILES):
                        transpose_tile(k)
                        if k >= 2:
                            products(k - 2)
                        if not first:
                            after(k)
                    for k in (NTILES - 2, NTILES - 1):
                        take(pe, tile_out[k % 2])
                        ins = products(k)
                    ins.then_inc(sums_done, 1)

                take(pe, ident_ready)
                window_sums(True)
                with pe.Fori(1, WINDOWS):
                    window_sums(False)
                take(pe, agg_ready)
                for k in range(NTILES):
                    after(k)

            @block.scalar
            def _(act):
                def load_state(v):
                    act.dma_start(h[:, :], window(state_d, v)).then_inc(h_in, 16)
                    act.dma_start(res[:, :, :], windows_of(rows_d)[v]).then_inc(res_in, 16)

                def after(k, v, last=False):
                    if k == GATES + 4:
                        take(act, gates_done)
                        act.activation(r_g[:, :], gates_ps[0][:, 0:WN], ACT.Sigmoid, bias=f.b[:, L, 1:2])
                        act.activation(z_g[:, :], gates_ps[1][:, 0:WN], ACT.Sigmoid, bias=f.b[:, L, 2:3]).then_inc(rz_ready, 1)
                    if k == GATES + 10:
                        take(act, pre_n)
                        act.activation(n_g[:, :], t_g[:, :], ACT.Tanh, bias=f.b[:, L, 3:4]).then_inc(n_ready, 1)
                    if k == BACK + 8:
                        act_norm(act)
                        if not last:
                            load_state(v + 1)
                    if k == STORE:
                        take(act, rows_ready)
                        act.dma_start(windows_of(out)[v], rows[:, :, :]).then_inc(rows_out, 16)

                def tiles(v=None):
                    for k in range(0, NTILES, 2):
                        take(act, tile_done[0])
                        act.copy(turned[k % 4][:, :], turn[0][0:NT, 0:WN]).then_inc(tile_out[0], 1)
                        if v is not None:
                            after(k, v)
                    act_sums(act)

                load_state(0)
                tiles()
                with act.Fori(1, WINDOWS) as v:
                    tiles(v - 1)
                for k in range(0, NTILES, 2):
                    after(k, WINDOWS - 1, True)

            @block.vector
            def _(dve):
                def after(k):
                    if k == KINDS_TURN + 3:
                        take(dve, kindT_done)
                        dve.tensor_copy(kindT[:, :], gates_ps[0][0:TC, 0:WN]).then_inc(kindT_ready, 1)
                    if k == EMBED + 3:
                        take(dve, embed_done)
                        dve.tensor_tensor(agg[:, :], agg_msgs[:, :], gates_ps[1][:, 0:WN], ALU.add).then_inc(agg_full, 1)
                    if k == GATES + 7:
                        take(dve, rz_ready)
                        dve.scalar_tensor_tensor(out=d_g[:, :], in0=gates_ps[3][:, 0:WN], scalar=f.b[:, L, 6:7], in1=r_g[:, :],
                                                 op0=ALU.add, op1=ALU.mult).then_inc(own, 1)
                        take(dve, own)
                        dve.tensor_tensor(t_g[:, :], d_g[:, :], gates_ps[2][:, 0:WN], ALU.add).then_inc(pre_n, 1)
                    if k == GATES + 13:
                        take(dve, n_ready)
                        dve.tensor_tensor(d_g[:, :], h[:, :], n_g[:, :], ALU.subtract).then_inc(own, 1)
                        take(dve, own)
                        dve.tensor_tensor(t_g[:, :], d_g[:, :], z_g[:, :], ALU.mult).then_inc(own, 1)
                        take(dve, own)
                        dve.tensor_tensor(new[:, :], t_g[:, :], n_g[:, :], ALU.add).then_inc(new_ready, 1)
                    if k == BACK + 5:
                        dve_norm(dve, gates_ps[0]).then_inc(rows_ready, 1)

                def sum_kinds():
                    dve.drain()
                    dve.tensor_reduce(kind_sums[:, :, :], kinds[:, :, :, :].rearrange("p w g t -> p g t w"), AX.X, ALU.add).then_inc(kinds_ready, 1)

                def tiles(post):
                    if post:
                        sum_kinds()
                    for k in range(1, NTILES, 2):
                        take(dve, tile_done[1])
                        dve.tensor_copy(turned[k % 4][:, :], turn[1][0:NT, 0:WN]).then_inc(tile_out[1], 1)
                        if (k + 1) % (PART * WT) == 0:
                            i = k // (PART * WT)
                            dve.drain()
                            dve.tensor_copy(kinds[:, i * PART:(i + 1) * PART, :, :],
                                            strips[i][0:NT, :, :, :].bitcast(F8)[:, :, :, WN:TILE]).then_inc(load_free, 1)
                        if post:
                            after(k)
                    if post:
                        take(dve, rows_out, 16)
                    take(dve, high_out)
                    dve.scalar_tensor_tensor(out=agg_msgs[:, :], in0=low_ps[:, 0:WN], scalar=1.0 / LOW, in1=high[:, :],
                                             op0=ALU.mult, op1=ALU.add).then_inc(agg_ready, 1)

                dve.tensor_copy(ident16[:, :], f.ident[0:NT, 0:NT]).then_inc(ident_ready, 1)
                dve.sem_inc(load_free, SLOTS)
                tiles(False)
                with dve.Fori(1, WINDOWS):
                    tiles(True)
                sum_kinds()
                for k in range(1, NTILES, 2):
                    after(k)
                take(dve, rows_out, 16)


def gnn_kernel(nc, x, xT, src, dst, etype, W0, W1, b0, b1, bm0, bm1, emb, out):
    with ExitStack() as ctx:
        f = Fast()

        def sb(name, shape, dt=F32):
            return ctx.enter_context(nc.sbuf_tensor(name, shape, dt))

        def sem(name):
            return ctx.enter_context(nc.semaphore(name))

        f.ident, f.zeros, f.ones = sb("f_ident", [P, P]), sb("f_zeros", [1, P]), sb("f_ones", [P, 1])
        f.general = sb("general", [1, 1], I32)
        f.tiles_d = nc.dram_tensor("adjacency", [WINDOWS, P, NTILES * WORDS], U32, kind="Internal").ap()
        f.w, f.b = sb("f_w", [H, 2, 7 * H]), sb("f_b", [H, 2, 7])
        f.b_msg, f.emb = sb("f_b_msg", [P, 2, H]), sb("f_emb", [TC, H])
        f.w_ih = lambda layer, gate: f.w[:, layer, H * (1 + gate):H * (2 + gate)]
        f.w_hh = lambda layer, gate: f.w[:, layer, H * (4 + gate):H * (5 + gate)]
        diff = sb("f_diff", [P, P], I32)
        diff_ready, zeroed, weights_in, made = sem("diff_ready"), sem("emb_zeroed"), sem("weights_in"), sem("made")
        with nc.Block() as block:
            @block.sync
            def _(sp):
                for i, (W, b, bm) in enumerate(((W0, b0, bm0), (W1, b1, bm1))):
                    sp.dma_start(f.w[:, i, :], W).then_inc(weights_in, 16)
                    sp.dma_start(f.b[:, i, :], b).then_inc(weights_in, 16)
                    sp.dma_start(f.b_msg[:, i, :], bm.to_broadcast([P, H])).then_inc(weights_in, 16)
                sp.wait_ge(zeroed, 1)
                sp.dma_start(f.emb[0:TYPES, :], emb).then_inc(weights_in, 16)
                sp.wait_ge(weights_in, 112)

            @block.gpsimd
            def _(pool):
                pool.memset(f.emb[:, :], 0.0).then_inc(zeroed, 1)
                pool.iota(diff[:, :], [[1, P]], base=0, channel_multiplier=-1).then_inc(diff_ready, 1)

            @block.vector
            def _(dve):
                dve.memset(f.zeros[:, :], 0.0)
                dve.memset(f.ones[:, :], 1.0)
                dve.wait_ge(diff_ready, 1)
                dve.tensor_scalar(f.ident[:, :], diff[:, :], 0.0, None, ALU.is_equal).then_inc(made, 1)
                dve.wait_ge(weights_in, 112)
                dve.tensor_tensor(f.b[:, :, 1:3], f.b[:, :, 1:3], f.b[:, :, 4:6], ALU.add).then_inc(made, 1)
                dve.wait_ge(made, 2)
        jobs = ExitStack()
        f.job_from, f.job_to, f.job_kind = (jobs.enter_context(nc.sbuf_tensor(n, [P, JC * P], F16))
                                            for n in ("job_from", "job_to", "job_kind"))
        find_jobs(nc, f, src, dst, etype)
        general = nc.values_load(f.general[0:1, 0:1])
        with nc.If(general != 0):
            general_path(nc, x, src, dst, etype, W0, W1, b0, b1, bm0, bm1, emb, out)
        with nc.Else():
            build(nc, f)
            jobs.close()
            network(nc, f, x, xT, out)


def kernel(x, src, dst, edge_type_9, L0_gnn_W_msg, L0_gnn_b_msg, L0_gnn_W_ih, L0_gnn_W_hh, L0_gnn_b_ih, L0_gnn_b_hh,
           L1_gnn_W_msg, L1_gnn_b_msg, L1_gnn_edge_embed, L1_gnn_W_ih, L1_gnn_W_hh, L1_gnn_b_ih, L1_gnn_b_hh):
    import numpy as np
    import concourse.bacc as bacc
    from concourse import mybir
    from concourse.bass_utils import run_bass_kernel_spmd

    def weights(msg, ih, hh):
        return np.concatenate([np.asarray(a).T for a in (msg, ih, hh)], axis=1)

    def biases(msg, ih, hh):
        return np.concatenate([np.asarray(a).reshape(-1, H) for a in (msg, ih, hh)]).T

    arrays = {
        "x": np.asarray(x),
        "xT": np.asarray(x).T,
        "src": np.asarray(src).reshape(EC, CHUNKS),
        "dst": np.asarray(dst).reshape(EC, CHUNKS),
        "etype": np.asarray(edge_type_9).reshape(EC, CHUNKS),
        "W0": weights(L0_gnn_W_msg, L0_gnn_W_ih, L0_gnn_W_hh),
        "W1": weights(L1_gnn_W_msg, L1_gnn_W_ih, L1_gnn_W_hh),
        "b0": biases(L0_gnn_b_msg, L0_gnn_b_ih, L0_gnn_b_hh),
        "b1": biases(L1_gnn_b_msg, L1_gnn_b_ih, L1_gnn_b_hh),
        "bm0": np.asarray(L0_gnn_b_msg).reshape(1, H),
        "bm1": np.asarray(L1_gnn_b_msg).reshape(1, H),
        "emb": np.asarray(L1_gnn_edge_embed),
    }
    arrays = {f"in_{k}": np.ascontiguousarray(a) for k, a in arrays.items()}
    nc = bacc.Bacc("TRN2", target_bir_lowering=False, num_devices=1)
    args = [nc.dram_tensor(k, a.shape, mybir.dt.from_np(a.dtype), kind="ExternalInput").ap() for k, a in arrays.items()]
    out = nc.dram_tensor("out_0", (NODES, H), mybir.dt.float32, kind="ExternalOutput").ap()
    gnn_kernel(nc, *args, out)
    r = run_bass_kernel_spmd(nc, [arrays], core_ids=[0])
    return r.results[0]["out_0"]
```

```python
from contextlib import ExitStack

import concourse.bass as bass
from concourse import mybir

ALU = mybir.AluOpType
ACT = mybir.ActivationFunctionType
AX = mybir.AxisListType
F32 = mybir.dt.float32
F16 = mybir.dt.float16
F8 = mybir.dt.float8e4
I32 = mybir.dt.int32
U32 = mybir.dt.uint32

NODES = 12500
EDGES = 212500
H = 128
TYPES = 9
TC = 12
NT = 125
NTILES = NODES // NT
WT = 4
WN = NT * WT
WINDOWS = NODES // WN
EC = 125
CHUNKS = EDGES // EC
STEPS = 5
EPS = 1e-5
FAR = 1 << 20

def general_path(nc, x, src, dst, etype, W0, W1, b0, b1, bm0, bm1, emb, out):
    with ExitStack() as ctx:
        def sb(name, shape, dt=F32):
            return ctx.enter_context(nc.sbuf_tensor(name, shape, dt))

        def psum(name, shape, dt=F32):
            return ctx.enter_context(nc.psum_tensor(name, shape, dt))

        def sem(name):
            return ctx.enter_context(nc.semaphore(name))

        rows = nc.dram_tensor("state", [NODES, H], F32, kind="Internal").ap()
        sums = nc.dram_tensor("edge_sums", [NODES, H + TC], F32, kind="Internal").ap()

        ident = sb("ident", [128, 128])
        lower = sb("lower", [EC, EC])
        zeros = sb("zeros", [NT, H + TC])
        iota_t = sb("iota_t", [EC, TC])
        iota_i = sb("iota_i", [128, 128], I32)
        w_sb = sb("w_sb", [H, 2, 7 * H])
        b_sb = sb("b_sb", [H, 2, 7])
        emb_sb = sb("emb_sb", [TC, 2, H])
        bm_sb = sb("bm_sb", [TC, 2, H])
        src_sb = sb("src_sb", [EC, CHUNKS], I32)
        dst_sb = sb("dst_sb", [EC, CHUNKS], I32)
        typ_sb = sb("typ_sb", [EC, CHUNKS], I32)
        typ_f = sb("typ_f", [EC, CHUNKS])

        in_row = sb("in_row", [EC, 1], U32)
        out_row = sb("out_row", [EC, 1], U32)
        out_f = sb("out_f", [EC, 1])
        write_f = sb("write_f", [EC, 1])
        write_row = sb("write_row", [EC, 1], U32)
        same = sb("same", [EC, EC])
        scrap = sb("scrap", [EC, EC])
        dups = sb("dups", [EC, 1])
        msg = sb("msg", [EC, H + TC])
        msg_rows = sb("msg_rows", [EC, H])
        acc = sb("acc", [EC, H + TC])

        s_rows = sb("s_rows", [NT, WT, H + TC])
        h_rows = sb("h_rows", [NT, WT, H])
        hT = sb("hT", [H, WN])
        sT = sb("sT", [H, WN])
        cT = sb("cT", [TC, WN])
        agg = sb("agg", [H, WN])
        r_g = sb("r_g", [H, WN])
        z_g = sb("z_g", [H, WN])
        n_g = sb("n_g", [H, WN])
        t_g = sb("t_g", [H, WN])
        d_g = sb("d_g", [H, WN])
        new_T = sb("new_T", [H, WN])
        res = sb("res", [NT, WT, H])
        new_rows = sb("new_rows", [NT, WT, H])
        stats = sb("stats", [NT, WT, 6])
        mv = sb("mv", [NT, WT, 2])
        var = sb("var", [NT, WT])
        std = sb("std", [NT, WT])
        rstd = sb("rstd", [NT, WT])

        banks = [psum(f"bank{i}", [128, 512]) for i in range(8)]

        loaded = sem("loaded")
        consts = sem("consts")
        vc = sem("vc")
        emb_zero = sem("emb_zero")

        def w_ih(layer, gate):
            return w_sb[:, layer, H * (1 + gate):H * (2 + gate)]

        def w_hh(layer, gate):
            return w_sb[:, layer, H * (4 + gate):H * (5 + gate)]

        with nc.Block() as block:
            @block.sync
            def _(sp):
                for i, W in enumerate((W0, W1)):
                    sp.dma_start(w_sb[:, i, :], W).then_inc(loaded, 16)
                for i, b in enumerate((b0, b1)):
                    sp.dma_start(b_sb[:, i, :], b).then_inc(loaded, 16)
                sp.wait_ge(emb_zero, 1)
                sp.dma_start(emb_sb[0:TYPES, 1, :], emb).then_inc(loaded, 16)
                sp.dma_start(bm_sb[:, 0, :], bm0.to_broadcast([TC, H])).then_inc(loaded, 16)
                sp.dma_start(bm_sb[:, 1, :], bm1.to_broadcast([TC, H])).then_inc(loaded, 16)
                sp.dma_start(src_sb[:, :], src).then_inc(loaded, 16)
                sp.dma_start(dst_sb[:, :], dst).then_inc(loaded, 16)
                sp.dma_start(typ_sb[:, :], etype).then_inc(loaded, 16)
                sp.dma_start(rows, x).then_inc(loaded, 16)
                sp.wait_ge(loaded, 176)

            @block.gpsimd
            def _(pool):
                pool.memset(emb_sb[:, :, :], 0.0).then_inc(emb_zero, 1)
                pool.iota(iota_i[:, :], [[1, 128]], base=0, channel_multiplier=-1).then_inc(consts, 1)

            @block.vector
            def _(dve):
                dve.memset(zeros[:, :], 0.0)
                dve.wait_ge(consts, 1)
                dve.tensor_copy(ident[:, :], iota_i[:, :]).then_inc(vc, 1)
                dve.wait_ge(vc, 1)
                dve.tensor_scalar(lower[:, :], ident[0:EC, 0:EC], 0.0, None, ALU.is_lt).then_inc(vc, 1)
                dve.wait_ge(vc, 2)
                dve.tensor_scalar(ident[:, :], ident[:, :], 0.0, None, ALU.is_equal).then_inc(vc, 1)
                dve.wait_ge(loaded, 176)
                dve.tensor_copy(typ_f[:, :], typ_sb[:, :]).then_inc(vc, 1)
                dve.wait_ge(vc, 4)
                dve.tensor_scalar(typ_f[:, :], typ_f[:, :], 0.0, float(TYPES - 1), ALU.max, ALU.min).then_inc(vc, 1)
                dve.tensor_tensor(b_sb[:, :, 1:3], b_sb[:, :, 1:3], b_sb[:, :, 4:6], ALU.add).then_inc(vc, 1)
                dve.wait_ge(emb_zero, 1)
                dve.tensor_tensor(emb_sb[:, :, :], emb_sb[:, :, :], bm_sb[:, :, :], ALU.add).then_inc(vc, 1)
                dve.wait_ge(vc, 7)

        iota_ready = sem("iota_ready")
        with nc.Block() as block:
            @block.gpsimd
            def _(pool):
                pool.iota(iota_i[0:EC, 0:TC], [[1, TC]], base=0, channel_multiplier=0).then_inc(iota_ready, 1)

            @block.vector
            def _(dve):
                dve.wait_ge(iota_ready, 1)
                dve.tensor_copy(iota_t[:, :], iota_i[0:EC, 0:TC]).then_inc(vc, 1)
                dve.wait_ge(vc, 8)

        def take(eng, sem, n=1):
            eng.wait_ge(sem, n)
            eng.sem_inc(sem, -n)

        (idx_pool, idx_pe, msg_in, acc_in, scattered, acc_done, idx_used, bcast, same_ready, sel_done,
         zeroed, dve_own) = (sem(n) for n in
            ("idx_pool", "idx_pe", "msg_in", "acc_in", "scattered", "acc_done", "idx_used", "bcast",
             "same_ready", "sel_done", "zeroed", "dve_own"))
        sums_clear = sem("sums_clear")

        def sum_edges(layer, in_sb, out_sb):
            with nc.Block() as block:
                @block.sync
                def _(sp):
                    by_tile = sums.rearrange("(a p) f -> a p f", p=NT)
                    with sp.Fori(0, NTILES // 4) as a:
                        for t in range(4):
                            sp.dma_start(by_tile[a * 4 + t], zeros[:, :]).then_inc(zeroed, 16)
                        take(sp, zeroed, 64)
                    sp.sem_inc(sums_clear, 1)

                @block.gpsimd
                def _(pool):
                    take(pool, sums_clear)
                    with pool.Fori(0, CHUNKS):
                        take(pool, idx_pool, 2)
                        pool.indirect_dma_start(msg_rows[:, :], None, rows,
                                                bass.IndirectOffsetOnAxis(ap=in_row[:, :], axis=0)).then_inc(msg_in, 16)
                        pool.indirect_dma_start(acc[:, :], None, sums,
                                                bass.IndirectOffsetOnAxis(ap=out_row[:, :], axis=0)).then_inc(acc_in, 16)
                        take(pool, acc_done, 2)
                        pool.indirect_dma_start(sums, bass.IndirectOffsetOnAxis(ap=write_row[:, :], axis=0),
                                                acc[:, :], None, bounds_check=NODES - 1, oob_is_err=False).then_inc(scattered, 16)
                        pool.wait_ge(scattered, 16)
                        pool.inc_swdge_sem([msg_in, acc_in, scattered], [16, 16, 16], mode="sub")
                        pool.sem_inc(idx_used, 1)

                @block.vector
                def _(dve):
                    dve.sem_inc(idx_used, 1)
                    with dve.Fori(0, CHUNKS) as c:
                        take(dve, idx_used)
                        dve.tensor_copy(out_f[:, :], out_sb[:, bass.ds(c, 1)]).then_inc(idx_pe, 1)
                        dve.tensor_copy(in_row[:, :], in_sb[:, bass.ds(c, 1)]).then_inc(idx_pool, 1)
                        dve.tensor_copy(out_row[:, :], out_sb[:, bass.ds(c, 1)]).then_inc(idx_pool, 1)
                        if layer:
                            dve.tensor_scalar(msg[:, H:H + TC], iota_t[:, :], typ_f[:, bass.ds(c, 1)], None, ALU.is_equal).then_inc(dve_own, 1)
                        else:
                            dve.tensor_scalar(msg[:, H:H + TC], iota_t[:, :], 0.0, None, ALU.is_equal).then_inc(dve_own, 1)
                        take(dve, bcast)
                        dve.tensor_scalar(same[:, :], banks[0][0:EC, 0:EC], out_f[:, :], None, ALU.is_equal).then_inc(dve_own, 1)
                        dve.wait_ge(dve_own, 2)
                        dve.tensor_tensor(scrap[:, :], same[:, :], lower[:, :], ALU.mult).then_inc(dve_own, 1)
                        dve.wait_ge(dve_own, 3)
                        dve.tensor_reduce(dups[:, :], scrap[:, :], mybir.AxisListType.X, ALU.max).then_inc(dve_own, 1)
                        dve.wait_ge(dve_own, 4)
                        dve.scalar_tensor_tensor(out=write_f[:, :], in0=dups[:, :], scalar=float(FAR), in1=out_f[:, :],
                                                 op0=ALU.mult, op1=ALU.add).then_inc(dve_own, 1)
                        take(dve, dve_own, 5)
                        dve.tensor_copy(write_row[:, :], write_f[:, :]).then_inc(acc_done, 1)
                        dve.wait_ge(msg_in, 16)
                        dve.tensor_copy(msg[:, 0:H], msg_rows[:, :]).then_inc(same_ready, 1)
                        take(dve, sel_done)
                        dve.wait_ge(acc_in, 16)
                        dve.tensor_tensor(acc[:, :], acc[:, :], banks[1][0:EC, 0:H + TC], ALU.add).then_inc(acc_done, 1)
                    take(dve, idx_used)

                @block.tensor
                def _(pe):
                    with pe.Fori(0, CHUNKS):
                        take(pe, idx_pe)
                        pe.transpose(banks[0][0:EC, 0:EC], out_f[:, 0:1].to_broadcast([EC, EC]), ident[0:EC, 0:EC]).then_inc(bcast, 1)
                        take(pe, same_ready)
                        pe.matmul(banks[1][0:EC, 0:H + TC], same[:, :], msg[:, :], start=True, stop=True).then_inc(sel_done, 1)

        (win_in, h_in, res_in, turned, s_done, agg_ps, agg_sb, gates_ps, rz_done, pre_n, n_done, new_done, back_ps,
         var_done, std_done, rows_done, stored) = (sem(n) for n in
            ("win_in", "h_in", "res_in", "turned", "s_done", "agg_ps", "agg_sb", "gates_ps", "rz_done", "pre_n", "n_done",
             "new_done", "back_ps", "var_done", "std_done", "rows_done", "stored"))

        def windows(a):
            return a.rearrange("(w t p) f -> w p t f", t=WT, p=NT)

        def gru(L, residual, result):
            with nc.Block() as block:
                @block.sync
                def _(sp):
                    with sp.Fori(0, WINDOWS) as w:
                        sp.dma_start(s_rows[:, :, :], windows(sums)[w]).then_inc(win_in, 16)
                        sp.dma_start(h_rows[:, :, :], windows(rows)[w]).then_inc(h_in, 16)
                        if residual is not None:
                            sp.dma_start(res[:, :, :], windows(residual)[w]).then_inc(res_in, 16)
                        take(sp, rows_done)
                        sp.dma_start(windows(result)[w], new_rows[:, :, :]).then_inc(stored, 16)
                        take(sp, stored, 16)

                @block.tensor
                def _(pe):
                    with pe.Fori(0, WINDOWS):
                        take(pe, win_in, 16)
                        take(pe, h_in, 16)
                        for t in range(WT):
                            node = slice(t * NT, (t + 1) * NT)
                            pe.transpose(banks[0][:, node], s_rows[:, t, 0:H], ident[0:NT, 0:NT])
                            pe.transpose(banks[1][0:TC, node], s_rows[:, t, H:H + TC], ident[0:NT, 0:NT])
                            mm = pe.transpose(banks[7][:, node], h_rows[:, t, :], ident[0:NT, 0:NT])
                        mm.then_inc(turned, 1)
                        take(pe, s_done)
                        pe.matmul(banks[2][:, 0:WN], w_sb[:, L, 0:H], sT[:, :], start=True, stop=False)
                        pe.matmul(banks[2][:, 0:WN], emb_sb[:, L, :], cT[:, :], start=False, stop=True).then_inc(agg_ps, 1)
                        take(pe, agg_sb)
                        for g in range(2):
                            pe.matmul(banks[3 + g][:, 0:WN], w_ih(L, g), agg[:, :], start=True, stop=False)
                            pe.matmul(banks[3 + g][:, 0:WN], w_hh(L, g), hT[:, :], start=False, stop=True)
                        pe.matmul(banks[5][:, 0:WN], w_ih(L, 2), agg[:, :], start=True, stop=True)
                        pe.matmul(banks[6][:, 0:WN], w_hh(L, 2), hT[:, :], start=True, stop=True).then_inc(gates_ps, 1)
                        take(pe, new_done)
                        for t in range(WT):
                            mm = pe.transpose(banks[0][0:NT, t * H:(t + 1) * H], new_T[:, t * NT:(t + 1) * NT], ident[:, :])
                        mm.then_inc(back_ps, 1)

                @block.scalar
                def _(act):
                    with act.Fori(0, WINDOWS):
                        take(act, gates_ps)
                        act.activation(r_g[:, :], banks[3][:, 0:WN], ACT.Sigmoid, bias=b_sb[:, L, 1:2])
                        act.activation(z_g[:, :], banks[4][:, 0:WN], ACT.Sigmoid, bias=b_sb[:, L, 2:3]).then_inc(rz_done, 1)
                        take(act, pre_n)
                        act.activation(n_g[:, :], t_g[:, :], ACT.Tanh, bias=b_sb[:, L, 3:4]).then_inc(n_done, 1)
                        if residual is not None:
                            take(act, var_done)
                            act.activation(std[:, :], var[:, :], ACT.Sqrt).then_inc(std_done, 1)

                @block.vector
                def _(dve):
                    with dve.Fori(0, WINDOWS):
                        take(dve, turned)
                        dve.tensor_copy(sT[:, :], banks[0][:, 0:WN])
                        dve.tensor_copy(hT[:, :], banks[7][:, 0:WN])
                        dve.tensor_copy(cT[:, :], banks[1][0:TC, 0:WN]).then_inc(s_done, 1)
                        take(dve, agg_ps)
                        dve.tensor_copy(agg[:, :], banks[2][:, 0:WN]).then_inc(agg_sb, 1)
                        take(dve, rz_done)
                        dve.scalar_tensor_tensor(out=t_g[:, :], in0=banks[6][:, 0:WN], scalar=b_sb[:, L, 6:7], in1=r_g[:, :],
                                                 op0=ALU.add, op1=ALU.mult).then_inc(dve_own, 1)
                        take(dve, dve_own)
                        dve.tensor_tensor(t_g[:, :], t_g[:, :], banks[5][:, 0:WN], ALU.add).then_inc(pre_n, 1)
                        take(dve, n_done)
                        dve.tensor_tensor(d_g[:, :], hT[:, :], n_g[:, :], ALU.subtract).then_inc(dve_own, 1)
                        take(dve, dve_own)
                        dve.tensor_tensor(d_g[:, :], d_g[:, :], z_g[:, :], ALU.mult).then_inc(dve_own, 1)
                        take(dve, dve_own)
                        dve.tensor_tensor(new_T[:, :], d_g[:, :], n_g[:, :], ALU.add).then_inc(new_done, 1)
                        take(dve, back_ps)
                        back = banks[0][0:NT, 0:WT * H].rearrange("p (t f) -> p t f", t=WT)
                        if residual is None:
                            dve.tensor_copy(new_rows[:, :, :], back).then_inc(rows_done, 1)
                            return
                        take(dve, res_in, 16)
                        dve.tensor_tensor(res[:, :, :], res[:, :, :], back, ALU.add).then_inc(dve_own, 1)
                        take(dve, dve_own)
                        for t in range(WT):
                            last = dve.bn_stats(stats[:, t, :], res[:, t, :])
                        last.then_inc(dve_own, 1)
                        take(dve, dve_own)
                        for t in range(WT):
                            last = dve.bn_aggr(mv[:, t, :], stats[:, t, :])
                        last.then_inc(dve_own, 1)
                        take(dve, dve_own)
                        dve.tensor_scalar(var[:, :], mv[:, :, 1], EPS, None, ALU.add).then_inc(var_done, 1)
                        take(dve, std_done)
                        dve.reciprocal(rstd[:, :], std[:, :]).then_inc(dve_own, 1)
                        take(dve, dve_own)
                        for t in range(WT):
                            last = dve.tensor_scalar(new_rows[:, t, :], res[:, t, :], mv[:, t, 0:1], rstd[:, t:t + 1],
                                                     ALU.subtract, ALU.mult)
                        last.then_inc(rows_done, 1)

        with nc.Fori(0, STEPS - 1):
            sum_edges(0, dst_sb, src_sb)
            gru(0, None, rows)
        sum_edges(0, dst_sb, src_sb)
        gru(0, x, rows)
        sum_edges(1, src_sb, dst_sb)
        gru(1, rows, out)


P = 128
COLS = 2048
KEYS = P * COLS
ROWS = KEYS // P
RUN = 16
BLOCKS = WINDOWS * NTILES
HALF = BLOCKS // 2
CODE_SHIFT, FROM_SHIFT, TO_SHIFT = 20, 13, 4
PAD_CODE = 2008
JOB_COLS = -(-BLOCKS // P)
EXTRA = JOB_COLS
JC = JOB_COLS + 1
WJ = NTILES + WT
TILE = 512


LOW = 2048.0


class Fast:
    pass


def take(eng, sem, n=1):
    eng.wait_ge(sem, n)
    eng.sem_inc(sem, -n)


def find_jobs(nc, f, src, dst, etype, xT):
    with ExitStack() as ctx:
        def sb(name, shape, dt=F32):
            return ctx.enter_context(nc.sbuf_tensor(name, shape, dt))

        def sem(name):
            return ctx.enter_context(nc.semaphore(name))

        banks = [ctx.enter_context(nc.psum_tensor(f"sort_bank{i}", [P, 512], F32)) for i in range(8)]
        bufs = [sb("keys_a", [P, COLS]), sb("keys_b", [P, COLS])]
        making = ExitStack()

        def made(name, dt=F32):
            return making.enter_context(nc.sbuf_tensor(name, [EC, CHUNKS], dt))

        lane = sb("lane", [P, 1], I32)
        bits = sb("bits", [P, 8], I32)
        sign = sb("sign", [P, 9])
        flip = sb("flip", [P, 8])
        x_win = [sb(f"x_win{i}", [H, WN]) for i in range(2)]
        ones_row, minus = sb("ones_row", [1, NT]), sb("minus_ident", [NT, NT], F16)
        msg_bank = banks[6:8]

        raw = [made(n, I32) for n in ("raw_from", "raw_to", "raw_kind")]
        fl = [made(f"fl{i}") for i in range(8)]
        integer, low = made("integer", I32), made("low", I32)

        keys_d = nc.dram_tensor("sorted_keys", [ROWS + 1, P], F32, kind="Internal").ap()
        firsts_d = nc.dram_tensor("first_keys", [ROWS], F32, kind="Internal").ap()

        edges_in, own, sign_ready = sem("edges_in"), sem("own"), sem("sign_ready")
        to_pe, on_psum, off_psum = sem("to_pe"), sem("on_psum"), sem("off_psum")

        first_made, first_high, first_rest = sem("first_made"), sem("first_high"), sem("first_rest")
        x_in, x_used, bank_free = ([sem(f"{n}{i}") for i in range(2)] for n in ("x_in", "x_used", "bank_free"))
        key_u = bufs[0][:, :].bitcast(U32)

        with nc.Block() as block:
            @block.sync
            def _(sp):
                for t, d in zip(raw, (dst, src, etype)):
                    sp.dma_start(t[:, :], d).then_inc(edges_in, 16)
                sp.wait_ge(edges_in, 48)

            @block.gpsimd
            def _(pool):
                pool.iota(lane[:, :], [[1, 1]], base=0, channel_multiplier=1).then_inc(sign_ready, 1)
                pool.memset(bufs[0][:, :].bitcast(I32), PAD_CODE << CODE_SHIFT).then_inc(sign_ready, 1)
                pool.wait_ge(sign_ready, 2)
                pool.memset(f.msgs0[96:P, :, :, :], 0.0)

            @block.vector
            def _(dve):
                n = 0

                def step(ins):
                    nonlocal n
                    n += 1
                    ins.then_inc(own, 1)
                    dve.wait_ge(own, n)

                def floor_div(out, x, d):
                    step(dve.tensor_scalar(fl[6][:, :], x, 0.5, 1.0 / d, ALU.add, ALU.mult))
                    step(dve.tensor_copy(integer[:, :], fl[6][:, :]))
                    step(dve.tensor_copy(out, integer[:, :]))
                    step(dve.tensor_tensor(fl[7][:, :], out, fl[6][:, :], ALU.is_gt))
                    step(dve.tensor_tensor(out, out, fl[7][:, :], ALU.subtract))

                frm, to, kind, tile, window, tmp = (t[:, :] for t in fl[0:6])
                dve.wait_ge(edges_in, 48)
                step(dve.tensor_copy(frm, raw[0][:, :]))
                step(dve.tensor_copy(to, raw[1][:, :]))
                step(dve.tensor_copy(kind, raw[2][:, :]))
                step(dve.tensor_scalar(kind, kind, 0.0, float(TYPES - 1), ALU.max, ALU.min))
                floor_div(tile, frm, NT)
                floor_div(window, to, WN)
                step(dve.scalar_tensor_tensor(out=frm, in0=tile, scalar=-float(NT), in1=frm, op0=ALU.mult, op1=ALU.add))
                step(dve.scalar_tensor_tensor(out=to, in0=window, scalar=-float(WN), in1=to, op0=ALU.mult, op1=ALU.add))
                step(dve.scalar_tensor_tensor(out=kind, in0=to, scalar=float(1 << TO_SHIFT), in1=kind, op0=ALU.mult, op1=ALU.add))
                step(dve.scalar_tensor_tensor(out=kind, in0=frm, scalar=float(1 << FROM_SHIFT), in1=kind, op0=ALU.mult, op1=ALU.add))
                step(dve.tensor_copy(low[:, :], kind))
                step(dve.scalar_tensor_tensor(out=tile, in0=window, scalar=-float(WT), in1=tile, op0=ALU.mult, op1=ALU.add))
                step(dve.tensor_scalar(tmp, tile, 0.0, float(NTILES), ALU.is_lt, ALU.mult))
                step(dve.tensor_tensor(tile, tile, tmp, ALU.add))
                step(dve.scalar_tensor_tensor(out=tile, in0=window, scalar=float(NTILES), in1=tile, op0=ALU.mult, op1=ALU.add))
                block_code(dve, step, tile, window, tmp, frm)
                step(dve.tensor_copy(integer[:, :], frm))
                dve.wait_ge(sign_ready, 2)
                step(dve.tensor_scalar(integer[:, :], integer[:, :], CODE_SHIFT, None, ALU.logical_shift_left))
                step(dve.tensor_tensor(bufs[0][0:EC, 0:CHUNKS].bitcast(I32), integer[:, :], low[:, :], ALU.bitwise_or))
                step(dve.memset(sign[:, :], 1.0))
                for b in range(7):
                    step(dve.tensor_scalar(bits[:, b:b + 1], lane[:, :], b, 1, ALU.logical_shift_right, ALU.bitwise_and))
                    step(dve.tensor_scalar(sign[:, b + 1:b + 2], bits[:, b:b + 1], -2.0, 1.0, ALU.mult, ALU.add))
                step(dve.tensor_tensor(flip[:, :], sign[:, 1:9], sign[:, 0:8], ALU.mult))
                step(dve.memset(ones_row[:, :], 1.0))
                step(dve.tensor_scalar(minus[:, :], f.ident[0:NT, 0:NT], -1.0, None, ALU.mult))
                dve.sem_inc(own, -n)

        making.close()

        NAT = COLS.bit_length() - 1
        ALL = KEYS.bit_length() - 1
        BANK = 512
        sorted_in = []

        def pairs(buf, j, cols=slice(0, COLS)):
            return buf[:, cols].rearrange("p (a t d) -> p a t d", t=2, d=1 << j)

        with nc.Block() as block:
            @block.vector
            def _(dve):
                n, evicted, cur = 0, 0, 0

                def step(*instructions):
                    nonlocal n
                    n += 1
                    instructions[-1].then_inc(own, 1)
                    dve.wait_ge(own, n)

                for k in range(1, NAT):
                    for j in reversed(range(k)):
                        v, o = (x[:, :].rearrange("p (a r b t d) -> p a r b t d", r=2, b=1 << (k - j - 1), t=2, d=1 << j)
                                for x in (bufs[cur], bufs[1 - cur]))
                        step(*[dve.tensor_tensor(o[:, :, r, :, t, :], v[:, :, r, :, 0, :], v[:, :, r, :, 1, :],
                                                 ALU.min if r == t else ALU.max)
                               for r in range(2) for t in range(2)])
                        cur = 1 - cur
                for k in range(NAT, ALL + 1):
                    flipped = dve.tensor_scalar(bufs[1 - cur][:, :], bufs[cur][:, :], flip[:, k - NAT:k - NAT + 1], None, ALU.mult)
                    cur = 1 - cur
                    if k == NAT:
                        step(flipped)
                    else:
                        flipped.then_inc(to_pe, 4)
                        cur = 1 - cur
                        for j in reversed(range(NAT, k)):
                            first, last = j == k - 1, j == NAT
                            if first or last:
                                for b in range(4):
                                    c = slice(b * BANK, (b + 1) * BANK)
                                    if first:
                                        dve.wait_ge(off_psum, evicted + b + 1)
                                    v, o = pairs(bufs[cur], j - NAT, c), pairs(bufs[1 - cur], j - NAT, c)
                                    dve.tensor_tensor(o[:, :, 0, :], v[:, :, 0, :], v[:, :, 1, :], ALU.min)
                                    ins = dve.tensor_tensor(o[:, :, 1, :], v[:, :, 0, :], v[:, :, 1, :], ALU.max)
                                    if last:
                                        ins.then_inc(to_pe, 1)
                                if not last:
                                    step(ins)
                            else:
                                v, o = pairs(bufs[cur], j - NAT), pairs(bufs[1 - cur], j - NAT)
                                step(dve.tensor_tensor(o[:, :, 0, :], v[:, :, 0, :], v[:, :, 1, :], ALU.min),
                                     dve.tensor_tensor(o[:, :, 1, :], v[:, :, 0, :], v[:, :, 1, :], ALU.max))
                            cur = 1 - cur
                        evicted += 8
                        dve.wait_ge(off_psum, evicted)
                        cur = 1 - cur
                    for j in reversed(range(NAT)):
                        v, o = pairs(bufs[cur], j), pairs(bufs[1 - cur], j)
                        step(dve.tensor_tensor(o[:, :, 0, :], v[:, :, 0, :], v[:, :, 1, :], ALU.min),
                             dve.tensor_tensor(o[:, :, 1, :], v[:, :, 0, :], v[:, :, 1, :], ALU.max))
                        cur = 1 - cur
                sorted_in.append(cur)

            def sources():
                cur = (NAT - 1) * NAT // 2 % 2
                for k in range(NAT, ALL + 1):
                    cur = 1 - cur
                    if k > NAT:
                        yield cur
                        cur = 1 - cur
                        cur = (cur + k - NAT) % 2
                        yield cur
                        cur = 1 - cur
                    cur = (cur + NAT) % 2

            UNROLL = 5

            def of_window(half, w):
                return f.msgs0[0:NT, bass.ds(w * WT, WT), half, :]

            @block.sync
            def _(sp):
                for used in x_used:
                    sp.sem_inc(used, 1)
                with sp.Fori(0, WINDOWS // UNROLL) as r:
                    for i in range(UNROLL):
                        take(sp, x_used[i % 2])
                        sp.dma_start(x_win[i % 2][:, :], xT[:, bass.ds(r * (UNROLL * WN) + i * WN, WN)]).then_inc(x_in[i % 2], 16)
                for used in x_used:
                    take(sp, used)

            @block.tensor
            def _(pe):
                with pe.Fori(0, WINDOWS // UNROLL) as r:
                    for i in range(UNROLL):
                        take(pe, x_in[i % 2], 16)
                        take(pe, bank_free[i % 2])
                        for t in range(WT):
                            out = msg_bank[i % 2][0:NT, t * H:(t + 1) * H]
                            pe.matmul(out, x_win[i % 2][:, t * NT:(t + 1) * NT], f.w[:, 0, 0:H], start=t == 0, stop=False, skip_group_check=True)
                            ins = pe.matmul(out, ones_row[:, :], f.b_msg[0:1, 0, :], start=False, stop=True, skip_group_check=True)
                        ins.then_inc(first_made, 1)
                        take(pe, first_high)
                        pe.sem_inc(x_used[i % 2], 1)
                        pe.matmul(msg_bank[i % 2][0:NT, :], minus[:, :], of_window(0, r * UNROLL + i), start=False, stop=True,
                                  skip_group_check=True).then_inc(first_rest, 1)
                for free in bank_free:
                    take(pe, free)
                for turn, cur in enumerate(sources()):
                    for b in range(4):
                        pe.wait_ge(to_pe, turn * 4 + b + 1)
                        for i in range(4 * b, 4 * b + 4):
                            ins = pe.transpose(banks[b][:, (i % 4) * P:(i % 4 + 1) * P], bufs[cur][:, i * P:(i + 1) * P], f.ident[:, :])
                        ins.then_inc(on_psum, 1)

            @block.scalar
            def _(act):
                for free in bank_free:
                    act.sem_inc(free, 1)
                with act.Fori(0, WINDOWS // UNROLL) as r:
                    for i in range(UNROLL):
                        by_tile = msg_bank[i % 2][0:NT, :].rearrange("p (t f) -> p t f", t=WT)
                        take(act, first_made)
                        act.copy(of_window(0, r * UNROLL + i), by_tile).then_inc(first_high, 1)
                        take(act, first_rest)
                        act.activation(of_window(1, r * UNROLL + i), by_tile, ACT.Copy, scale=LOW).then_inc(bank_free[i % 2], 1)
                for turn, cur in enumerate(sources()):
                    for b in range(4):
                        act.wait_ge(on_psum, turn * 4 + b + 1)
                        act.copy(bufs[1 - cur][:, b * BANK:(b + 1) * BANK], banks[b][:, :]).then_inc(off_psum, 1)

        f.keys, f.spare = bufs[sorted_in[0]], bufs[1 - sorted_in[0]]
        f.keys_d, f.firsts_d = keys_d, firsts_d
        cut_jobs(nc, f, sem, sb, banks)


def block_code(dve, step, number, neg, tmp, out):
    step(dve.tensor_scalar(neg, number, float(HALF), None, ALU.is_lt))
    step(dve.tensor_scalar(tmp, number, -1.0, float(HALF - 1), ALU.mult, ALU.add))
    step(dve.tensor_scalar(number, number, -float(HALF), None, ALU.add))
    step(dve.tensor_tensor(out, number, tmp, ALU.max))
    step(dve.scalar_tensor_tensor(out=out, in0=neg, scalar=2048.0, in1=out, op0=ALU.mult, op1=ALU.add))
    step(dve.tensor_scalar(out, out, 8.0, None, ALU.add))


def cut_jobs(nc, f, sem, sb, banks):
    firsts = sb("firsts", [P, ROWS])
    shifted = sb("shifted", [P, COLS])
    scrap = sb("scrap_n", [P, COLS])
    number = sb("number", [P, JC])
    number_i = sb("number_i", [P, JC], I32)
    t1, t2, code, rounded = (sb(n, [P, JC]) for n in ("t1", "t2", "code", "rounded"))
    code_i, low_i, rows_i = sb("code_i", [P, JC], I32), sb("low_i", [P, JC], I32), sb("rows_i", [P, 2, JC + 1], U32)
    lo = sb("lo", [P, JC])
    passed = sb("passed", [P, JC])
    start = sb("start", [P, JC])
    row_a = sb("row_a", [P, JC + 1, P])
    row_b = sb("row_b", [P, JC, P])
    field = sb("field", [P, JC, P])
    field_i = sb("field_i", [P, JC, P], I32)
    mask = sb("mask", [P, JC, P], I32)
    match = sb("match", [P, JC, P])
    lanes = sb("lanes", [P, P])
    sums = sb("sums", [P, 2])
    bad = sb("bad", [1, 2])
    stored, firsts_in, shifted_in = sem("stored_keys"), sem("firsts_in"), sem("shifted_in")
    iota_in, rows_ready, rows_in, rows2_in = sem("iota_in"), sem("rows_ready"), sem("rows_in"), sem("rows2_in")
    own, fields, turned, moved, total = sem("own2"), sem("fields"), sem("turned2"), sem("moved"), sem("total")
    field_used = sem("field_used")
    n_pads = KEYS - EDGES

    with nc.Block() as block:
        @block.sync
        def _(sp):
            with nc.allow_non_contiguous_dma(reason="one key of each row"):
                sp.dma_start(f.firsts_d.rearrange("(p a) -> p a", p=P), f.keys[:, 0:COLS:P]).then_inc(stored, 16)
            sp.dma_start(f.keys_d[0:ROWS].rearrange("(p a) b -> p (a b)", p=P), f.keys[:, :]).then_inc(stored, 16)
            sp.dma_start(f.keys_d[ROWS:ROWS + 1, :], f.zeros[0:1, 0:P]).then_inc(stored, 16)
            sp.wait_ge(stored, 48)
            sp.dma_start(firsts[:, :], f.firsts_d.rearrange("(a b) -> a b", a=1).to_broadcast([P, ROWS])).then_inc(firsts_in, 16)
            flat = f.keys_d.rearrange("a b -> (a b)")
            sp.dma_start(shifted[:, :], flat[RUN:RUN + KEYS].rearrange("(p c) -> p c", p=P)).then_inc(shifted_in, 16)
            sp.wait_ge(shifted_in, 16)

        @block.gpsimd
        def _(pool):
            pool.iota(number_i[:, 0:EXTRA], [[P, JOB_COLS]], base=0, channel_multiplier=1)
            pool.iota(number_i[:, EXTRA:JC], [[0, 1]], base=0, channel_multiplier=1).then_inc(iota_in, 1)
            pool.wait_ge(iota_in, 1)
            pool.iota(field_i[:, 0, :], [[1, P]], base=0, channel_multiplier=0).then_inc(iota_in, 1)
            pool.wait_ge(rows_ready, 1)
            pool.wait_ge(stored, 48)

            def gather(out, index, sem_in):
                pool.indirect_dma_start(out, None, f.keys_d, bass.IndirectOffsetOnAxis(ap=index, axis=0)).then_inc(sem_in, 16)

            for c in range(JC):
                gather(row_a[:, c, :], rows_i[:, 0, c:c + 1], rows_in)
            gather(row_a[:, JC, :], rows_i[:, 1, EXTRA:JC], rows2_in)
            for c in range(JC):
                gather(row_b[:, c, :], rows_i[:, 1, c:c + 1] if c < EXTRA else rows_i[:, 1, JC:JC + 1], rows2_in)

        @block.vector
        def _(dve):
            n = 0

            def step(ins):
                nonlocal n
                n += 1
                ins.then_inc(own, 1)
                dve.wait_ge(own, n)

            def bc(x, cols=JC):
                return x[:, 0:cols].unsqueeze(2).to_broadcast([P, cols, P])

            dve.wait_ge(iota_in, 2)
            step(dve.tensor_copy(number[:, :], number_i[:, :]))
            step(dve.tensor_copy(lanes[:, :], field_i[:, 0, :]))
            e = slice(EXTRA, JC)
            step(dve.tensor_scalar(t1[:, e], number[:, e], 0.5, 1.0 / WT, ALU.add, ALU.mult))
            step(dve.tensor_copy(code_i[:, e], t1[:, e]))
            step(dve.tensor_copy(rounded[:, e], code_i[:, e]))
            step(dve.tensor_tensor(t2[:, e], rounded[:, e], t1[:, e], ALU.is_gt))
            step(dve.tensor_tensor(rounded[:, e], rounded[:, e], t2[:, e], ALU.subtract))
            step(dve.scalar_tensor_tensor(out=number[:, e], in0=rounded[:, e], scalar=float(NTILES - WT), in1=number[:, e],
                                          op0=ALU.mult, op1=ALU.add))
            block_code(dve, step, number[:, :], t1[:, :], t2[:, :], code[:, :])
            step(dve.tensor_copy(code_i[:, :], code[:, :]))
            step(dve.tensor_scalar(t1[:, :], t1[:, :], float((1 << CODE_SHIFT) - 1), None, ALU.mult))
            step(dve.tensor_copy(low_i[:, :], t1[:, :]))
            step(dve.tensor_scalar(code_i[:, :], code_i[:, :], CODE_SHIFT, None, ALU.logical_shift_left))
            step(dve.tensor_tensor(lo[:, :].bitcast(I32), code_i[:, :], low_i[:, :], ALU.bitwise_or))
            dve.wait_ge(firsts_in, 16)
            for c in range(JC):
                step(dve.tensor_scalar(scrap[:, :], firsts[:, :], lo[:, c:c + 1], None, ALU.is_lt, ALU.add,
                                       accum_out=passed[:, c:c + 1]))
            step(dve.tensor_scalar(t1[:, :], passed[:, :], -1.0, 0.0, ALU.add, ALU.max))
            step(dve.tensor_copy(rows_i[:, 0, 0:JC], t1[:, :]))
            step(dve.tensor_scalar(t2[:, :], t1[:, :], 1.0, float(ROWS - 1), ALU.add, ALU.min))
            step(dve.tensor_copy(rows_i[:, 1, 0:JC], t2[:, :]))
            step(dve.tensor_scalar(t2[:, e], t1[:, e], 2.0, float(ROWS - 1), ALU.add, ALU.min))
            step(dve.tensor_copy(rows_i[:, 1, JC:JC + 1], t2[:, e]))
            dve.sem_inc(rows_ready, 1)

            a, b = f.keys[:, :].bitcast(I32), shifted[:, :].bitcast(I32)
            dve.wait_ge(shifted_in, 16)
            step(dve.tensor_scalar(f.spare[:, :].bitcast(I32), a, FROM_SHIFT, None, ALU.logical_shift_right))
            step(dve.tensor_scalar(b, b, FROM_SHIFT, None, ALU.logical_shift_right))
            step(dve.tensor_tensor(scrap[:, :], f.spare[:, :].bitcast(I32), b, ALU.is_equal))
            step(dve.tensor_reduce(sums[:, 1:2], scrap[:, :], AX.X, ALU.add))

            dve.wait_ge(rows_in, 16 * JC)
            step(dve.tensor_tensor(field[:, :, :], row_a[:, 0:JC, :], bc(lo), ALU.is_lt))
            step(dve.tensor_reduce(start[:, :], field[:, :, :], AX.X, ALU.add))
            step(dve.tensor_tensor(mask[:, :, :], lanes[:, :].unsqueeze(1).to_broadcast([P, JC, P]), bc(start), ALU.is_ge))
            dve.wait_ge(rows2_in, 16 * (JC + 1))
            step(dve.tensor_copy(row_a[:, EXTRA, :], row_a[:, JC, :]))
            step(dve.copy_predicated(row_b[:, :, :], mask[:, :, :], row_a[:, 0:JC, :]))
            key = row_b[:, :, :].bitcast(I32)
            step(dve.tensor_scalar(field_i[:, :, :], key, CODE_SHIFT, (1 << 12) - 1, ALU.logical_shift_right, ALU.bitwise_and))
            step(dve.tensor_tensor(match[:, :, :], field_i[:, :, :], bc(code), ALU.is_equal))
            step(dve.tensor_reduce(sums[:, 0:1], match[:, :, :], AX.XY, ALU.add))
            step(dve.tensor_scalar(field_i[:, :, :], key, FROM_SHIFT, 127, ALU.logical_shift_right, ALU.bitwise_and))
            step(dve.scalar_tensor_tensor(out=field[:, :, :], in0=field_i[:, :, :], scalar=1.0, in1=match[:, :, :],
                                          op0=ALU.add, op1=ALU.mult))
            dve.sem_inc(fields, 1)
            dve.wait_ge(field_used, 1)
            step(dve.tensor_scalar(field_i[:, :, :], key, TO_SHIFT, 511, ALU.logical_shift_right, ALU.bitwise_and))
            step(dve.tensor_copy(field[:, :, :], field_i[:, :, :]))
            dve.sem_inc(fields, 1)
            dve.wait_ge(field_used, 2)
            step(dve.tensor_scalar(field_i[:, :, :], key, 15, None, ALU.bitwise_and))
            step(dve.tensor_copy(field[:, :, :], field_i[:, :, :]))
            dve.sem_inc(fields, 1)
            dve.wait_ge(total, 1)
            step(dve.tensor_scalar(bad[:, 0:1], banks[7][0:1, 0:1], float(EDGES), None, ALU.not_equal))
            step(dve.tensor_scalar(bad[:, 1:2], banks[7][0:1, 1:2], float(n_pads - RUN), None, ALU.not_equal))
            step(dve.tensor_tensor(f.general[:, :], bad[:, 0:1], bad[:, 1:2], ALU.max))

        @block.tensor
        def _(pe):
            m = 0
            for i in range(3):
                pe.wait_ge(fields, i + 1)
                for c0 in range(0, JC, 4):
                    if m >= 7:
                        pe.wait_ge(moved, m - 6)
                    for c in range(c0, min(c0 + 4, JC)):
                        ins = pe.transpose(banks[m % 7][:, (c - c0) * P:(c - c0 + 1) * P], field[:, c, :], f.ident[:, :])
                    ins.then_inc(turned, 1)
                    m += 1
            pe.matmul(banks[7][0:1, 0:2], f.ones[:, 0:1], sums[:, :], start=True, stop=True).then_inc(total, 1)

        @block.scalar
        def _(act):
            m = 0
            for i, out in enumerate((f.job_from, f.job_to, f.job_kind)):
                for c0 in range(0, JC, 4):
                    width = (min(c0 + 4, JC) - c0) * P
                    act.wait_ge(turned, m + 1)
                    act.activation(out[:, c0 * P:c0 * P + width], banks[m % 7][:, 0:width], ACT.Copy,
                                   bias=-1.0 if i == 0 else 0.0).then_inc(moved, 1)
                    m += 1
                    if m % -(-JC // 4) == 0:
                        act.wait_ge(moved, m)
                        act.sem_inc(field_used, 1)


GROUP = WT
GROUPS = NTILES // GROUP
LOAD = 10
LOADS = NTILES // LOAD
SLOTS = 5
BATCH = 8
RING = 13
WORDS = TILE // 4


def windows_of(a):
    return a.rearrange("(w t p) f -> w p t f", t=WT, p=NT)


def network(nc, f, x, xT, out):
    with ExitStack() as ctx:
        def sb(name, shape, dt=F32):
            return ctx.enter_context(nc.sbuf_tensor(name, shape, dt))

        def sem(name):
            return ctx.enter_context(nc.semaphore("net_" + name))

        banks = [ctx.enter_context(nc.psum_tensor(f"net_bank{i}", [P, TILE], F32)) for i in range(4)]
        pair = [ctx.enter_context(nc.psum_tensor(f"net_pair{i}", [P, 2, TILE], F32)) for i in range(2)]
        halves = [[p[:, i, :] for i in range(2)] for p in pair]
        sums_ps, gates_ps = (banks[0:2], halves[0]), banks[2:4] + halves[1]
        msg_ps, turn_ps = gates_ps[0], gates_ps[1]

        msgs = [f.msgs0, sb("messages1", [P, NTILES, 2, H], F16)]
        h, agg, high = sb("h_win", [H, WN]), sb("agg_win", [H, WN]), sb("high_win", [H, WN])
        r_g, z_g, n_g, t_g, d_g, new = (sb(n + "_win", [H, WN]) for n in ("r", "z", "n", "t", "d", "new"))
        msg, rest = sb("msg_win", [NT, WT, H]), sb("rest_win", [NT, WT, H])
        res, rows = sb("res_win", [NT, WT, H]), sb("rows_win", [NT, WT, H])
        stats, mv = sb("stats_win", [NT, WT, 6]), sb("mv_win", [NT, WT, 2])
        var, std, rstd = (sb(n + "_win", [NT, WT]) for n in ("var", "std", "rstd"))

        (h_in, res_in, sums_done, high_out, agg_ready, gates_done, rz_ready, pre_n, n_ready, new_ready, back_done,
         var_ready, std_ready, rows_ready, yT_done, yT_ready, msg_done, msg_ready, high_ready, rest_ready, state_out,
         rows_out, own) = (sem(n) for n in
            ("h_in", "res_in", "sums_done", "high_out", "agg_ready", "gates_done", "rz_ready", "pre_n", "n_ready", "new_ready",
             "back_done", "var_ready", "std_ready", "rows_ready", "yT_done", "yT_ready", "msg_done", "msg_ready", "high_ready",
             "rest_ready", "state_out", "rows_out", "own"))
        load_free = [sem(f"load_free{i}") for i in range(SLOTS)]
        load_in = [sem(f"load_in{i}") for i in range(SLOTS)]

        state_d = nc.dram_tensor("state_T", [H, NODES], F32, kind="Internal").ap()
        rows_d = nc.dram_tensor("normed_rows", [NODES, H], F32, kind="Internal").ap()

        def window(a, w):
            return a[:, bass.ds(w * WN, WN)]

        def pe_messages(pe, Lm, of):
            for t in range(WT):
                ins = pe.matmul(msg_ps[0:NT, t * H:(t + 1) * H], of[:, t * NT:(t + 1) * NT], f.w[:, Lm, 0:H], start=True, stop=True)
            ins.then_inc(msg_done, 1)

        def by_tile(ps):
            return ps[0:NT, :].rearrange("p (t f) -> p t f", t=WT)

        def dve_messages(dve, Lm, to, w):
            take(dve, msg_done)
            dve.drain()
            dve.tensor_tensor(msg[:, :, :], by_tile(msg_ps), f.b_msg[0:NT, Lm, :].unsqueeze(1).to_broadcast([NT, WT, H]), ALU.add).then_inc(msg_ready, 1)
            take(dve, high_ready)
            dve.tensor_tensor(rest[:, :, :], msg[:, :, :], to[0:NT, bass.ds(w * WT, WT), 0, :], ALU.subtract).then_inc(rest_ready, 1)

        def act_messages(act, to, w, then=None):
            take(act, msg_ready)
            act.copy(to[0:NT, bass.ds(w * WT, WT), 0, :], msg[:, :, :]).then_inc(high_ready, 1)
            if then:
                then()
            take(act, rest_ready)
            act.activation(to[0:NT, bass.ds(w * WT, WT), 1, :], rest[:, :, :], ACT.Copy, scale=LOW)

        def pe_rz(pe, L):
            take(pe, h_in, 16)
            for g in range(2):
                pe.matmul(gates_ps[g][:, 0:WN], f.w_ih(L, g), agg[:, :], start=True, stop=False)
                ins = pe.matmul(gates_ps[g][:, 0:WN], f.w_hh(L, g), h[:, :], start=False, stop=True)
            return ins

        def pe_n(pe, L, ps_i, ps_h):
            pe.matmul(ps_i[:, 0:WN], f.w_ih(L, 2), agg[:, :], start=True, stop=True)
            return pe.matmul(ps_h[:, 0:WN], f.w_hh(L, 2), h[:, :], start=True, stop=True)

        def pe_gates(pe, L):
            pe_rz(pe, L)
            pe_n(pe, L, *gates_ps[2:4]).then_inc(gates_done, 1)

        def act_gates(act, L):
            take(act, gates_done)
            act.activation(r_g[:, :], gates_ps[0][:, 0:WN], ACT.Sigmoid, bias=f.b[:, L, 1:2])
            act.activation(z_g[:, :], gates_ps[1][:, 0:WN], ACT.Sigmoid, bias=f.b[:, L, 2:3]).then_inc(rz_ready, 1)
            take(act, pre_n)
            act.activation(n_g[:, :], t_g[:, :], ACT.Tanh, bias=f.b[:, L, 3:4]).then_inc(n_ready, 1)

        def dve_gated(dve, L, ps_h):
            dve.scalar_tensor_tensor(out=d_g[:, :], in0=ps_h[:, 0:WN], scalar=f.b[:, L, 6:7], in1=r_g[:, :],
                                     op0=ALU.add, op1=ALU.mult).then_inc(own, 1)

        def dve_pre_n(dve, ps_i):
            take(dve, own)
            dve.tensor_tensor(t_g[:, :], d_g[:, :], ps_i[:, 0:WN], ALU.add).then_inc(pre_n, 1)

        def dve_candidate(dve, L, ps_i, ps_h):
            dve_gated(dve, L, ps_h)
            dve_pre_n(dve, ps_i)

        def dve_difference(dve):
            take(dve, n_ready)
            dve.tensor_tensor(d_g[:, :], h[:, :], n_g[:, :], ALU.subtract).then_inc(own, 1)

        def dve_kept(dve):
            take(dve, own)
            dve.tensor_tensor(t_g[:, :], d_g[:, :], z_g[:, :], ALU.mult).then_inc(own, 1)

        def dve_new(dve):
            dve_difference(dve)
            dve_kept(dve)
            dve_together(dve)

        def dve_together(dve):
            take(dve, own)
            dve.tensor_tensor(new[:, :], t_g[:, :], n_g[:, :], ALU.add).then_inc(new_ready, 1)

        def dve_gates(dve, L):
            take(dve, rz_ready)
            dve_candidate(dve, L, *gates_ps[2:4])
            dve_new(dve)

        def pe_back(pe, bank):
            take(pe, new_ready)
            for t in range(WT):
                ins = pe.transpose(bank[0:NT, t * H:(t + 1) * H], new[:, t * NT:(t + 1) * NT], f.ident[:, :])
            ins.then_inc(back_done, 1)

        def dve_residual(dve, bank):
            take(dve, back_done)
            take(dve, res_in, 16)
            dve.tensor_tensor(msg[:, :, :], res[:, :, :], by_tile(bank), ALU.add).then_inc(own, 1)

        def dve_stats(dve):
            take(dve, own)
            for t in range(WT):
                last = dve.bn_stats(stats[:, t, :], msg[:, t, :])
            last.then_inc(own, 1)

        def dve_variance(dve):
            take(dve, own)
            for t in range(WT):
                last = dve.bn_aggr(mv[:, t, :], stats[:, t, :])
            last.then_inc(own, 1)
            take(dve, own)
            dve.tensor_scalar(var[:, :], mv[:, :, 1], EPS, None, ALU.add).then_inc(var_ready, 1)

        def dve_moments(dve, bank):
            dve_residual(dve, bank)
            dve_stats(dve)
            dve_variance(dve)

        def dve_normed(dve):
            take(dve, std_ready)
            dve.reciprocal(rstd[:, :], std[:, :]).then_inc(own, 1)
            take(dve, own)
            for t in range(WT):
                last = dve.tensor_scalar(rows[:, t, :], msg[:, t, :], mv[:, t, 0:1], rstd[:, t:t + 1], ALU.subtract, ALU.mult)
            last.then_inc(rows_ready, 1)

        def act_norm(act):
            take(act, var_ready)
            act.activation(std[:, :], var[:, :], ACT.Sqrt).then_inc(std_ready, 1)

        def act_sums(act, parity):
            take(act, sums_done)
            act.copy(high[:, :], sums_ps[parity][0][:, 0:WN]).then_inc(high_out, 1)

        def dve_sums(dve, parity):
            take(dve, high_out)
            dve.scalar_tensor_tensor(out=agg[:, :], in0=sums_ps[parity][1][:, 0:WN], scalar=1.0 / LOW, in1=high[:, :],
                                     op0=ALU.mult, op1=ALU.add).then_inc(agg_ready, 1)

        def load_tiles(sp, w, g):
            sp.dma_start(loads[g % SLOTS][:, :], f.tiles_d[w][:, g * LOAD * WORDS:(g + 1) * LOAD * WORDS]).then_inc(load_in[g % SLOTS], 16)

        def advance(current, following, norm):
            Lm = 1 if norm else 0

            with nc.Block() as block:
                @block.sync
                def _(sp):
                    with sp.Fori(0, WINDOWS - 1 if norm else WINDOWS) as w:
                        for g in range(LOADS):
                            take(sp, load_free[g % SLOTS])
                            if g + SLOTS < LOADS:
                                load_tiles(sp, w, g + SLOTS)
                            else:
                                load_tiles(sp, (w + 1) % WINDOWS, g + SLOTS - LOADS)
                    if norm:
                        for g in range(LOADS):
                            take(sp, load_free[g % SLOTS])
                            if g + SLOTS < LOADS:
                                load_tiles(sp, WINDOWS - 1, g + SLOTS)

                @block.tensor
                def _(pe):
                    def sums(parity, post):
                        for g in range(LOADS):
                            take(pe, load_in[g % SLOTS], 16)
                            for i in range(LOAD):
                                k = g * LOAD + i
                                counts = loads[g % SLOTS][0:NT, i * WORDS:(i + 1) * WORDS].bitcast(F8)[:, 0:WN]
                                for half, ps in enumerate(sums_ps[parity]):
                                    ins = pe.matmul(ps[:, 0:WN], msgs[current][0:NT, k, half, :], counts, start=k == 0, stop=k == NTILES - 1)
                            ins.then_inc(*((load_free[g % SLOTS], 1) if g < LOADS - 1 else (sums_done, 1)))
                            if post:
                                after(g)

                    def after(g):
                        if g == 0:
                            take(pe, agg_ready)
                            pe.sem_inc(load_free[-1], 1)
                            pe_gates(pe, 0)
                        if norm:
                            if g == 2:
                                pe_back(pe, gates_ps[2])
                            if g == 5:
                                take(pe, rows_ready)
                                for t in range(WT):
                                    ins = pe.transpose(turn_ps[:, t * NT:(t + 1) * NT], rows[:, t, :], f.ident[0:NT, 0:NT])
                                ins.then_inc(yT_done, 1)
                            if g == 6:
                                take(pe, yT_ready)
                                pe_messages(pe, Lm, new)
                        elif g == 3:
                            take(pe, new_ready)
                            pe_messages(pe, Lm, new)

                    sums(0, False)
                    with pe.Fori(0, WINDOWS // 2):
                        sums(1, True)
                        sums(0, True)
                    for g in range(LOADS):
                        after(g)

                @block.scalar
                def _(act):
                    def load_state(w):
                        act.dma_start(h[:, :], window(state_d, w)).then_inc(h_in, 16)
                        if norm:
                            act.dma_start(res[:, :, :], windows_of(x)[w]).then_inc(res_in, 16)

                    def post(w, last=False):
                        def move():
                            act.dma_start(window(state_d, w), new[:, :]).then_inc(state_out, 16)
                            if norm:
                                act.dma_start(windows_of(rows_d)[w], rows[:, :, :]).then_inc(rows_out, 16)
                            if not last:
                                load_state(w + 1)

                        act_gates(act, 0)
                        if norm:
                            act_norm(act)
                        act_messages(act, msgs[following], w, move)

                    load_state(0)
                    act_sums(act, 0)
                    with act.Fori(0, WINDOWS // 2) as pair:
                        post(pair * 2)
                        act_sums(act, 1)
                        post(pair * 2 + 1)
                        act_sums(act, 0)
                    post(WINDOWS - 1, True)

                @block.vector
                def _(dve):
                    def post(w):
                        dve.drain()
                        dve_gates(dve, 0)
                        if norm:
                            dve_moments(dve, gates_ps[2])
                            dve_normed(dve)
                            take(dve, yT_done)
                            dve.tensor_copy(new[:, :], turn_ps[:, 0:WN]).then_inc(yT_ready, 1)
                        dve_messages(dve, Lm, msgs[following], w)
                        take(dve, state_out, 16)
                        if norm:
                            take(dve, rows_out, 16)

                    dve_sums(dve, 0)
                    with dve.Fori(0, WINDOWS // 2) as pair:
                        post(pair * 2)
                        dve_sums(dve, 1)
                        post(pair * 2 + 1)
                        dve_sums(dve, 0)
                    post(WINDOWS - 1)

        def build_and_advance():
            with ExitStack() as building:
                def sb(name, shape, dt=F32):
                    return building.enter_context(nc.sbuf_tensor(name, shape, dt))

                col_i = sb("col_i", [P, TILE], I32)
                col = sb("col", [P, TILE], F16)
                col_b = sb("col_b", [P, P, BATCH], F16)
                from_w = sb("from_w", [P, WJ], F16)
                to_f, kind_f = sb("to_f", [P, WJ]), sb("kind_f", [P, WJ])
                hot_from = [sb(f"hot_from{i}", [P, P, BATCH], F16) for i in range(4)]
                hot_to = [sb(f"hot_to{i}", [P, TILE], F16) for i in range(RING)]
                strip = [sb(f"strip{i}", [P, GROUP * WORDS], U32) for i in range(SLOTS)]
                group_msgs = [sb(f"group_msgs{i}", [P, GROUP, 2, H], F16) for i in range(SLOTS)]

                (iota_in, b_own, hot_ready, hot_free, pair_ready, strip_ready, strip_free, strip_seen, summed, rz_done,
                 rz_taken, n_done) = (sem(n) for n in (
                    "iota_in", "b_own", "hot_ready", "hot_free", "pair_ready", "strip_ready", "strip_free", "strip_seen", "summed",
                    "rz_done", "rz_taken", "n_done"))
                pair_free = [sem("pair_free0"), sem("pair_free1")]
                strip_out, group_in = ([sem(f"{n}{i}") for i in range(SLOTS)] for n in ("strip_out", "group_in"))

                jobs = [(i, c) for i in range(WT) for c in (i, WT + i)] + [(i, WT + i) for i in range(WT, NTILES)]
                firsts = [n for n, (slot, _) in enumerate(jobs) if slot % 2 == 0 and (n == 0 or jobs[n - 1][0] != slot)]

                def says(u):
                    last = (firsts + [WJ])[u + 1] - 1 - RING
                    if last < 0:
                        return last // 2 + 1
                    return max(v for v in range(len(firsts)) if firsts[v] <= last) + 1

                def used_before(u):
                    return says(u) - (says(u - 1) if u else -PAIRS_BEHIND - 1)

                PAIRS_BEHIND = len(firsts) - 1 - says(len(firsts) - 1)

                batches = WJ // BATCH
                ring = [b % 3 for b in range(batches - 1)] + [3]
                BEHIND = 2
                PE_RZ, PE_N, PE_MSG = 1, 5, 12
                ACT_RZ, ACT_N, ACT_MSG = 2, 7, 13
                DVE_RZ, DVE_N, DVE_NEW, DVE_MSG = 4, 7, 9, 15

                with nc.Block() as block:
                    @block.gpsimd
                    def _(pool):
                        pool.iota(col_i[:, :], [[1, TILE]], base=0, channel_multiplier=0).then_inc(iota_in, 1)

                    @block.vector
                    def _(dve):
                        def window_jobs(w, post):
                            dve.drain()
                            for out, jobs_of in ((from_w, f.job_from), (kind_f, f.job_kind), (to_f, f.job_to)):
                                dve.tensor_copy(out[:, 0:WT], jobs_of[:, bass.ds(w * WT + EXTRA * P, WT)])
                                last = dve.tensor_copy(out[:, WT:WJ], jobs_of[:, bass.ds(w * NTILES, NTILES)])
                            last.then_inc(b_own, 1)
                            take(dve, b_own)
                            for n, (slot, c) in enumerate(jobs):
                                b, i = divmod(n, BATCH)
                                if i == 0:
                                    cols = slice(b * BATCH, (b + 1) * BATCH)
                                    dve.tensor_tensor(hot_from[ring[b]][:, :, :], col_b[:, :, :],
                                                      from_w[:, cols].unsqueeze(1).to_broadcast([P, P, BATCH]), ALU.is_equal)
                                if n in firsts and used_before(firsts.index(n)):
                                    take(dve, hot_free, used_before(firsts.index(n)))
                                dve.tensor_scalar(hot_to[n % RING][:, WN:TILE], col[:, 0:TC], kind_f[:, c:c + 1], None, ALU.is_equal)
                                dve.tensor_scalar(hot_to[n % RING][:, 0:WN], col[:, 0:WN], to_f[:, c:c + 1], None, ALU.is_equal).then_inc(hot_ready, 1)
                                if slot % GROUP == GROUP - 1 and (n == WJ - 1 or jobs[n + 1][0] != slot) and post:
                                    after(slot // GROUP, w - 1)

                        def after(g, w):
                            if g == 0:
                                dve_sums(dve, 0)
                            if g == DVE_RZ:
                                take(dve, rz_ready)
                                dve.sem_inc(rz_taken, 1)
                            if g == DVE_N:
                                take(dve, n_done)
                                dve_candidate(dve, 0, *gates_ps[0:2])
                            if g == DVE_NEW:
                                dve_new(dve)
                            if g == DVE_MSG:
                                dve_messages(dve, 0, msgs[1], w)
                                take(dve, state_out, 16)

                        take(dve, iota_in)
                        dve.tensor_copy(col[:, :], col_i[:, :])
                        dve.tensor_copy(col_b[:, :, :], col_i[:, 0:P].unsqueeze(2).to_broadcast([P, P, BATCH])).then_inc(b_own, 1)
                        take(dve, b_own)
                        dve.sem_inc(hot_free, PAIRS_BEHIND)
                        window_jobs(0, False)
                        with dve.Fori(1, WINDOWS) as w:
                            window_jobs(w, True)
                        take(dve, hot_free, PAIRS_BEHIND)
                        for g in range(GROUPS):
                            after(g, WINDOWS - 1)

                    @block.tensor
                    def _(pe):
                        def tiles(g):
                            for n, (slot, c) in enumerate(jobs):
                                if slot // GROUP != g:
                                    continue
                                b, i = divmod(c, BATCH)
                                half = slot // 2 % 2
                                out = pair[half][:, slot % 2, :]
                                start = n == 0 or jobs[n - 1][0] != slot
                                stop = n == WJ - 1 or jobs[n + 1][0] != slot
                                if start and slot % 2 == 0:
                                    take(pe, pair_free[half])
                                take(pe, hot_ready)
                                ins = pe.matmul(out, hot_from[ring[b]][:, :, i], hot_to[n % RING][:, :], start=start, stop=stop)
                                if n in firsts:
                                    ins.then_inc(hot_free, 1)
                                if stop and slot % 2 == 1:
                                    ins.then_inc(pair_ready, 1)

                        def sums(g):
                            take(pe, strip_seen)
                            take(pe, group_in[g % SLOTS], 16)
                            for i in range(GROUP):
                                counts = strip[g % SLOTS][0:NT, i * WORDS:(i + 1) * WORDS].bitcast(F8)[:, 0:WN]
                                for half, ps in enumerate(sums_ps[0]):
                                    ins = pe.matmul(ps[:, 0:WN], group_msgs[g % SLOTS][0:NT, i, half, :], counts,
                                                    start=g == 0 and i == 0, stop=g == GROUPS - 1 and i == GROUP - 1)
                            ins.then_inc(*((summed, 1) if g < GROUPS - 1 else (sums_done, 1)))

                        def after(g):
                            if g == 0:
                                take(pe, agg_ready)
                                pe.sem_inc(summed, 1)
                            if g == PE_RZ:
                                pe_rz(pe, 0).then_inc(rz_done, 1)
                            if g == PE_N:
                                take(pe, rz_taken)
                                pe_n(pe, 0, *gates_ps[0:2]).then_inc(n_done, 1)
                            if g == PE_MSG:
                                take(pe, new_ready)
                                pe_messages(pe, 0, new)

                        def window_sums(post):
                            for g in range(GROUPS):
                                tiles(g)
                                if post:
                                    after(g)
                                if g >= BEHIND:
                                    sums(g - BEHIND)
                            for g in range(GROUPS - BEHIND, GROUPS):
                                sums(g)

                        window_sums(False)
                        with pe.Fori(1, WINDOWS):
                            window_sums(True)
                        for g in range(GROUPS):
                            after(g)
                        for free in pair_free:
                            take(pe, free)

                    @block.scalar
                    def _(act):
                        def load_state(w):
                            act.dma_start(h[:, :], window(xT, w)).then_inc(h_in, 16)

                        def after(g, w, last=False):
                            def move():
                                act.dma_start(window(state_d, w), new[:, :]).then_inc(state_out, 16)
                                if not last:
                                    load_state(w + 1)

                            if g == ACT_RZ:
                                take(act, rz_done)
                                act.activation(r_g[:, :], gates_ps[0][:, 0:WN], ACT.Sigmoid, bias=f.b[:, 0, 1:2])
                                act.activation(z_g[:, :], gates_ps[1][:, 0:WN], ACT.Sigmoid, bias=f.b[:, 0, 2:3]).then_inc(rz_ready, 1)
                            if g == ACT_N:
                                take(act, pre_n)
                                act.activation(n_g[:, :], t_g[:, :], ACT.Tanh, bias=f.b[:, 0, 3:4]).then_inc(n_ready, 1)
                            if g == ACT_MSG:
                                act_messages(act, msgs[1], w, move)

                        def window_strips(w):
                            for g in range(GROUPS):
                                take(act, strip_free)
                                for half in range(2):
                                    take(act, pair_ready)
                                    words = strip[g % SLOTS][:, 2 * half * WORDS:2 * (half + 1) * WORDS]
                                    act.activation(words.bitcast(F8), pair[half][:, :, :].rearrange("p a b -> p (a b)"), ACT.Copy,
                                                   saturate=False).then_inc(strip_ready if half else pair_free[0], 1)
                                if w is not None:
                                    after(g, w)
                            act_sums(act, 0)

                        act.sem_inc(pair_free[0], 1)
                        act.sem_inc(strip_free, SLOTS)
                        load_state(0)
                        window_strips(None)
                        with act.Fori(1, WINDOWS) as w:
                            window_strips(w - 1)
                        for g in range(GROUPS):
                            after(g, WINDOWS - 1, True)
                        take(act, strip_free, SLOTS)

                    @block.sync
                    def _(sp):
                        sp.sem_inc(pair_free[1], 1)
                        with sp.Fori(0, WINDOWS) as w:
                            def sent(g):
                                take(sp, strip_out[g % SLOTS], 16)
                                take(sp, summed)
                                sp.sem_inc(strip_free, 1)

                            for g in range(GROUPS):
                                at = (w + g) % GROUPS * (GROUP * WORDS)
                                sp.dma_start(group_msgs[g % SLOTS][:, :, :, :], msgs[0][:, bass.ds((w + g) % GROUPS * GROUP, GROUP), :, :]).then_inc(group_in[g % SLOTS], 16)
                                take(sp, strip_ready)
                                sp.sem_inc(pair_free[1], 1)
                                sp.sem_inc(strip_seen, 1)
                                sp.dma_start(f.tiles_d[w][:, bass.ds(at, GROUP * WORDS)], strip[g % SLOTS][:, :]).then_inc(strip_out[g % SLOTS], 16)
                                if g >= SLOTS - 2:
                                    sent(g - SLOTS + 2)
                            for g in range(GROUPS - SLOTS + 2, GROUPS):
                                sent(g)

        build_and_advance()
        with ExitStack() as ring:
            loads = [ring.enter_context(nc.sbuf_tensor(f"load{i}", [P, LOAD * WORDS], U32)) for i in range(SLOTS)]
            with nc.Block() as block:
                @block.sync
                def _(sp):
                    for g in range(SLOTS):
                        load_tiles(sp, 0, g)
            advance(1, 0, False)
            with nc.Fori(0, STEPS // 2 - 1):
                advance(0, 1, False)
                advance(1, 0, False)
            advance(0, 1, True)

        PART = WINDOWS // SLOTS
        KINDS_TURN, EMBED, GATES, BACK, STORE = 6, 12, 18, 52, 84
        strips = [msgs[0][:, :, :, :].rearrange("p k t f -> p (k t f)").bitcast(U32)[:, i * PART * GROUP * WORDS:(i + 1) * PART * GROUP * WORDS]
                  .rearrange("p (w g c) -> p w g c", w=PART, g=GROUP) for i in range(SLOTS)]
        turned = [sb(f"turned{i}", [NT, WN], F16) for i in range(4)]
        ident16 = sb("ident16", [NT, NT], F16)
        kinds = sb("kinds", [NT, WINDOWS, GROUP, TC])
        kind_sums, kindT = sb("kind_sums", [NT, GROUP, TC]), sb("kindT", [TC, WN])
        agg_msgs = sb("agg_msgs", [H, WN])
        tile_done, tile_out = [sem("tile_done_act"), sem("tile_done_dve")], [sem("tile_out_act"), sem("tile_out_dve")]
        ident_ready = sem("ident_ready")
        kinds_ready, kindT_done, kindT_ready, embed_done, agg_full = (
            sem(n) for n in ("kinds_ready", "kindT_done", "kindT_ready", "embed_done", "agg_full"))
        turn, (high_ps, low_ps) = sums_ps[1], sums_ps[0]
        L = 1

        with nc.Block() as block:
            @block.sync
            def _(sp):
                by_node = f.tiles_d.rearrange("w p c -> p w c")
                with sp.Fori(0, WINDOWS) as v:
                    for i in range(SLOTS):
                        take(sp, load_free[i])
                        sp.dma_start(strips[i].rearrange("p w g c -> p w (g c)"),
                                     by_node[:, i * PART:(i + 1) * PART, bass.ds(v * GROUP * WORDS, GROUP * WORDS)]).then_inc(load_in[i], 16)
                for free in load_free:
                    take(sp, free)

            @block.tensor
            def _(pe):
                def transpose_tile(k):
                    w, a = divmod(k, WT)
                    if k % (PART * WT) == 0:
                        take(pe, load_in[w // PART], 16)
                    if k >= 2:
                        take(pe, tile_out[k % 2])
                    for g in range(GROUP):
                        counts = strips[w // PART][0:NT, w % PART, g, :].bitcast(F8)[:, a * NT:(a + 1) * NT]
                        ins = pe.matmul(turn[k % 2][0:NT, g * NT:(g + 1) * NT], counts, ident16[:, :], start=True, stop=True)
                    ins.then_inc(tile_done[k % 2], 1)

                def products(k):
                    for half, ps in enumerate((high_ps, low_ps)):
                        ins = pe.matmul(ps[:, 0:WN], msgs[1][0:NT, k, half, :], turned[k % 4][:, :], start=k == 0, stop=k == NTILES - 1)
                    return ins

                def after(k):
                    if k == KINDS_TURN:
                        take(pe, kinds_ready)
                        for g in range(GROUP):
                            ins = pe.transpose(gates_ps[0][0:TC, g * NT:(g + 1) * NT], kind_sums[:, g, :], f.ident[0:NT, 0:NT])
                        ins.then_inc(kindT_done, 1)
                    if k == EMBED:
                        take(pe, kindT_ready)
                        pe.matmul(gates_ps[1][:, 0:WN], f.emb[:, :], kindT[:, :], start=True, stop=True).then_inc(embed_done, 1)
                    if k == GATES:
                        take(pe, agg_full)
                        pe_rz(pe, L)
                    if k == GATES + 2:
                        pe_n(pe, L, *gates_ps[2:4]).then_inc(gates_done, 1)
                    if k == BACK:
                        pe_back(pe, gates_ps[0])

                def window_sums(first):
                    for k in range(NTILES):
                        transpose_tile(k)
                        if k == 2 and not first:
                            take(pe, agg_ready)
                        if k >= 2:
                            products(k - 2)
                        if not first:
                            after(k)
                    for k in (NTILES - 2, NTILES - 1):
                        take(pe, tile_out[k % 2])
                        ins = products(k)
                    ins.then_inc(sums_done, 1)

                take(pe, ident_ready)
                window_sums(True)
                with pe.Fori(1, WINDOWS):
                    window_sums(False)
                take(pe, agg_ready)
                for k in range(NTILES):
                    after(k)

            @block.scalar
            def _(act):
                def load_state(v):
                    act.dma_start(h[:, :], window(state_d, v)).then_inc(h_in, 16)
                    act.dma_start(res[:, :, :], windows_of(rows_d)[v]).then_inc(res_in, 16)

                def after(k, v, last=False):
                    if k == GATES + 4:
                        take(act, gates_done)
                        act.activation(r_g[:, :], gates_ps[0][:, 0:WN], ACT.Sigmoid, bias=f.b[:, L, 1:2])
                    if k == GATES + 6:
                        act.activation(z_g[:, :], gates_ps[1][:, 0:WN], ACT.Sigmoid, bias=f.b[:, L, 2:3]).then_inc(rz_ready, 1)
                    if k == GATES + 10:
                        take(act, pre_n)
                        act.activation(n_g[:, :], t_g[:, :], ACT.Tanh, bias=f.b[:, L, 3:4]).then_inc(n_ready, 1)
                    if k == BACK + 16:
                        act_norm(act)
                        if not last:
                            load_state(v + 1)
                    if k == STORE:
                        take(act, rows_ready)
                        act.dma_start(windows_of(out)[v], rows[:, :, :]).then_inc(rows_out, 16)

                def tiles(v=None):
                    for k in range(0, NTILES, 2):
                        take(act, tile_done[0])
                        act.copy(turned[k % 4][:, :], turn[0][0:NT, 0:WN]).then_inc(tile_out[0], 1)
                        if v is not None:
                            after(k, v)
                    act_sums(act, 0)

                load_state(0)
                tiles()
                with act.Fori(1, WINDOWS) as v:
                    tiles(v - 1)
                for k in range(0, NTILES, 2):
                    after(k, WINDOWS - 1, True)

            @block.vector
            def _(dve):
                def after(k):
                    if k == KINDS_TURN + 3:
                        take(dve, kindT_done)
                        dve.tensor_copy(kindT[:, :], gates_ps[0][0:TC, 0:WN]).then_inc(kindT_ready, 1)
                    if k == EMBED + 3:
                        take(dve, embed_done)
                        dve.tensor_tensor(agg[:, :], agg_msgs[:, :], gates_ps[1][:, 0:WN], ALU.add).then_inc(agg_full, 1)
                    if k == GATES + 7:
                        take(dve, rz_ready)
                        dve_gated(dve, L, gates_ps[3])
                    if k == GATES + 9:
                        dve_pre_n(dve, gates_ps[2])
                    if k == GATES + 15:
                        dve_difference(dve)
                    if k == GATES + 17:
                        dve_kept(dve)
                    if k == GATES + 19:
                        dve_together(dve)
                    if k == BACK + 5:
                        dve_residual(dve, gates_ps[0])
                    if k == BACK + 7:
                        dve_stats(dve)
                    if k == BACK + 9:
                        dve_variance(dve)
                    if k == BACK + 21:
                        dve_normed(dve)

                def sum_kinds():
                    dve.drain()
                    dve.tensor_reduce(kind_sums[:, :, :], kinds[:, :, :, :].rearrange("p w g t -> p g t w"), AX.X, ALU.add).then_inc(kinds_ready, 1)

                def tiles(post):
                    if post:
                        sum_kinds()
                    for k in range(1, NTILES, 2):
                        take(dve, tile_done[1])
                        dve.tensor_copy(turned[k % 4][:, :], turn[1][0:NT, 0:WN]).then_inc(tile_out[1], 1)
                        if (k + 1) % (PART * WT) == 0:
                            i = k // (PART * WT)
                            dve.drain()
                            dve.tensor_copy(kinds[:, i * PART:(i + 1) * PART, :, :],
                                            strips[i][0:NT, :, :, :].bitcast(F8)[:, :, :, WN:TILE]).then_inc(load_free[i], 1)
                        if post:
                            after(k)
                    if post:
                        take(dve, rows_out, 16)
                    take(dve, high_out)
                    dve.scalar_tensor_tensor(out=agg_msgs[:, :], in0=low_ps[:, 0:WN], scalar=1.0 / LOW, in1=high[:, :],
                                             op0=ALU.mult, op1=ALU.add).then_inc(agg_ready, 1)

                dve.tensor_copy(ident16[:, :], f.ident[0:NT, 0:NT]).then_inc(ident_ready, 1)
                for free in load_free:
                    dve.sem_inc(free, 1)
                tiles(False)
                with dve.Fori(1, WINDOWS):
                    tiles(True)
                sum_kinds()
                for k in range(1, NTILES, 2):
                    after(k)
                take(dve, rows_out, 16)


def gnn_kernel(nc, x, xT, src, dst, etype, W0, W1, b0, b1, bm0, bm1, emb, out):
    with ExitStack() as ctx:
        f = Fast()

        def sb(name, shape, dt=F32):
            return ctx.enter_context(nc.sbuf_tensor(name, shape, dt))

        def sem(name):
            return ctx.enter_context(nc.semaphore(name))

        f.ident, f.zeros, f.ones = sb("f_ident", [P, P]), sb("f_zeros", [1, P]), sb("f_ones", [P, 1])
        f.general = sb("general", [1, 1], I32)
        f.tiles_d = nc.dram_tensor("adjacency", [WINDOWS, P, NTILES * WORDS], U32, kind="Internal").ap()
        f.w, f.b = sb("f_w", [H, 2, 7 * H]), sb("f_b", [H, 2, 7])
        f.b_msg, f.emb = sb("f_b_msg", [P, 2, H]), sb("f_emb", [TC, H])
        f.w_ih = lambda layer, gate: f.w[:, layer, H * (1 + gate):H * (2 + gate)]
        f.w_hh = lambda layer, gate: f.w[:, layer, H * (4 + gate):H * (5 + gate)]
        diff = sb("f_diff", [P, P], I32)
        diff_ready, zeroed, weights_in, made = sem("diff_ready"), sem("emb_zeroed"), sem("weights_in"), sem("made")
        with nc.Block() as block:
            @block.sync
            def _(sp):
                for i, (W, b, bm) in enumerate(((W0, b0, bm0), (W1, b1, bm1))):
                    sp.dma_start(f.w[:, i, :], W).then_inc(weights_in, 16)
                    sp.dma_start(f.b[:, i, :], b).then_inc(weights_in, 16)
                    sp.dma_start(f.b_msg[:, i, :], bm.to_broadcast([P, H])).then_inc(weights_in, 16)
                sp.wait_ge(zeroed, 1)
                sp.dma_start(f.emb[0:TYPES, :], emb).then_inc(weights_in, 16)
                sp.wait_ge(weights_in, 112)

            @block.gpsimd
            def _(pool):
                pool.memset(f.emb[:, :], 0.0).then_inc(zeroed, 1)
                pool.iota(diff[:, :], [[1, P]], base=0, channel_multiplier=-1).then_inc(diff_ready, 1)

            @block.vector
            def _(dve):
                dve.memset(f.zeros[:, :], 0.0)
                dve.memset(f.ones[:, :], 1.0)
                dve.wait_ge(diff_ready, 1)
                dve.tensor_scalar(f.ident[:, :], diff[:, :], 0.0, None, ALU.is_equal).then_inc(made, 1)
                dve.wait_ge(weights_in, 112)
                dve.tensor_tensor(f.b[:, :, 1:3], f.b[:, :, 1:3], f.b[:, :, 4:6], ALU.add).then_inc(made, 1)
                dve.wait_ge(made, 2)
        f.msgs0 = sb("messages0", [P, NTILES, 2, H], F16)
        f.job_from, f.job_to, f.job_kind = (sb(n, [P, JC * P], F16) for n in ("job_from", "job_to", "job_kind"))
        find_jobs(nc, f, src, dst, etype, xT)
        general = nc.values_load(f.general[0:1, 0:1])
        with nc.If(general != 0):
            general_path(nc, x, src, dst, etype, W0, W1, b0, b1, bm0, bm1, emb, out)
        with nc.Else():
            network(nc, f, x, xT, out)


def kernel(x, src, dst, edge_type_9, L0_gnn_W_msg, L0_gnn_b_msg, L0_gnn_W_ih, L0_gnn_W_hh, L0_gnn_b_ih, L0_gnn_b_hh,
           L1_gnn_W_msg, L1_gnn_b_msg, L1_gnn_edge_embed, L1_gnn_W_ih, L1_gnn_W_hh, L1_gnn_b_ih, L1_gnn_b_hh):
    import numpy as np
    import concourse.bacc as bacc
    from concourse import mybir
    from concourse.bass_utils import run_bass_kernel_spmd

    def weights(msg, ih, hh):
        return np.concatenate([np.asarray(a).T for a in (msg, ih, hh)], axis=1)

    def biases(msg, ih, hh):
        return np.concatenate([np.asarray(a).reshape(-1, H) for a in (msg, ih, hh)]).T

    arrays = {
        "x": np.asarray(x),
        "xT": np.asarray(x).T,
        "src": np.asarray(src).reshape(EC, CHUNKS),
        "dst": np.asarray(dst).reshape(EC, CHUNKS),
        "etype": np.asarray(edge_type_9).reshape(EC, CHUNKS),
        "W0": weights(L0_gnn_W_msg, L0_gnn_W_ih, L0_gnn_W_hh),
        "W1": weights(L1_gnn_W_msg, L1_gnn_W_ih, L1_gnn_W_hh),
        "b0": biases(L0_gnn_b_msg, L0_gnn_b_ih, L0_gnn_b_hh),
        "b1": biases(L1_gnn_b_msg, L1_gnn_b_ih, L1_gnn_b_hh),
        "bm0": np.asarray(L0_gnn_b_msg).reshape(1, H),
        "bm1": np.asarray(L1_gnn_b_msg).reshape(1, H),
        "emb": np.asarray(L1_gnn_edge_embed),
    }
    arrays = {f"in_{k}": np.ascontiguousarray(a) for k, a in arrays.items()}
    nc = bacc.Bacc("TRN2", target_bir_lowering=False, num_devices=1)
    args = [nc.dram_tensor(k, a.shape, mybir.dt.from_np(a.dtype), kind="ExternalInput").ap() for k, a in arrays.items()]
    out = nc.dram_tensor("out_0", (NODES, H), mybir.dt.float32, kind="ExternalOutput").ap()
    gnn_kernel(nc, *args, out)
    r = run_bass_kernel_spmd(nc, [arrays], core_ids=[0])
    return r.results[0]["out_0"]
```
